# Optimizing a Trainium2 kernel written in Bass

```python
import numpy as np
import jax
import jax.numpy as jnp

def _softmax(x, axis=-1):
    return jax.nn.softmax(x, axis=axis)

def _gelu(x):
    return jax.nn.gelu(x, approximate=True)

def _silu(x):
    return jax.nn.silu(x)

def _sigmoid(x):
    return jax.nn.sigmoid(x)

def _layernorm(x, axis=-1, eps=1e-05):
    m = jnp.mean(x, axis=axis, keepdims=True)
    v = jnp.var(x, axis=axis, keepdims=True)
    return (x - m) / jnp.sqrt(v + eps)

def _scatter_add(tgt, idx, src, axis=0):
    return tgt.at[idx].add(src)

def _segment_sum(src, seg, n):
    return jax.ops.segment_sum(src, seg, n)
kernel_name = 'mk_recurrent_d1_jaxref_r8_bbd420'

def setup_inputs(seed: int=0):
    np.random.seed(seed)
    _w = jnp.asarray

    def _L0_attn_setup():
        import jax, jax.numpy as jnp
        import numpy as np
        B, S, E, H, Dh = (2, 256, 128, 16, 64)
        key = jax.random.key(seed)
        ks = jax.random.split(key, 8)
        w = 0.02
        return {'x': jax.random.normal(ks[0], (B, S, E), jnp.float32), 'Wq': jax.random.normal(ks[1], (H, Dh, E), jnp.float32) * w, 'bq': jax.random.normal(ks[2], (H, Dh), jnp.float32) * w, 'Wk': jax.random.normal(ks[3], (H, Dh, E), jnp.float32) * w, 'bk': jax.random.normal(ks[4], (H, Dh), jnp.float32) * w, 'Wv': jax.random.normal(ks[5], (H, Dh, E), jnp.float32) * w, 'bv': jax.random.normal(ks[6], (H, Dh), jnp.float32) * w, 'proj': jax.random.normal(ks[7], (H * Dh, E), jnp.float32) * w}
    _L0_attn_in = _L0_attn_setup()

    def _L0_ffn_setup():
        import jax, jax.numpy as jnp
        import numpy as np
        INT4_QMAX = 7.0

        def simulate_quantize_int4(w):
            scale = jnp.max(jnp.abs(w)) / INT4_QMAX
            q = jnp.clip(jnp.round(w / scale), -8.0, 7.0)
            return q * scale
        key = jax.random.key(seed)
        k_x, k_w, k_bias, k_a, k_b = jax.random.split(key, 5)
        d_in, features, rank = (128, 128, 16)
        x = jax.random.normal(k_x, (4, 1024, d_in), dtype=jnp.float32)
        kernel = jax.random.normal(k_w, (d_in, features), dtype=jnp.float32)
        bias = jax.random.normal(k_bias, (features,), dtype=jnp.float32)
        a = jax.random.normal(k_a, (d_in, rank), dtype=jnp.float32) * (1.0 / np.sqrt(d_in))
        b = jax.random.normal(k_b, (rank, features), dtype=jnp.float32) * 0.01
        return {'x': x, 'kernel': kernel, 'bias': bias, 'a': a, 'b': b}
    _L0_ffn_in = _L0_ffn_setup()
    _d = {'L0_attn_x': _L0_attn_in['x'], 'L0_attn_Wq': _L0_attn_in['Wq'], 'L0_attn_bq': _L0_attn_in['bq'], 'L0_attn_Wk': _L0_attn_in['Wk'], 'L0_attn_bk': _L0_attn_in['bk'], 'L0_attn_Wv': _L0_attn_in['Wv'], 'L0_attn_bv': _L0_attn_in['bv'], 'L0_attn_proj': _L0_attn_in['proj'], 'L0_ffn_kernel': _L0_ffn_in['kernel'], 'L0_ffn_bias': _L0_ffn_in['bias'], 'L0_ffn_a': _L0_ffn_in['a'], 'L0_ffn_b': _L0_ffn_in['b']}
    _x0 = _d['L0_attn_x']
    _d['L0_attn_x'] = jax.random.normal(jax.random.fold_in(jax.random.key(seed), 1), (4, 1024, 128), dtype=_x0.dtype)
    del _x0
    return _d

def reference(L0_attn_x, L0_attn_Wq, L0_attn_bq, L0_attn_Wk, L0_attn_bk, L0_attn_Wv, L0_attn_bv, L0_attn_proj, L0_ffn_kernel, L0_ffn_bias, L0_ffn_a, L0_ffn_b):

    def _L0_attn_ref(x, Wq, bq, Wk, bk, Wv, bv, proj):
        import jax, jax.numpy as jnp
        import numpy as np
        B, S, E, H, Dh = (2, 256, 128, 16, 64)
        b, s, e = x.shape
        h, dh, _ = Wq.shape
        scale = jnp.sqrt(jnp.asarray(dh, x.dtype))
        q = jnp.einsum('bse,hde->bhsd', x, Wq) + bq[None, :, None, :]
        k = jnp.einsum('bse,hde->bhsd', x, Wk) + bk[None, :, None, :]
        v = jnp.einsum('bse,hde->bhsd', x, Wv) + bv[None, :, None, :]
        causal = jnp.triu(jnp.ones((s, s), bool), 1)
        scores = jnp.einsum('bhsd,bhtd->bhst', q, k) / scale
        scores = jnp.where(causal[None, None], -jnp.inf, scores)
        att = jax.nn.softmax(scores, axis=-1) / scale
        z = jnp.einsum('bhst,bhtd->bhsd', att, v)
        z = z.reshape(b, s, h * dh)
        return z @ proj

    def _L0_ffn_ref(x, kernel, bias, a, b):
        import jax, jax.numpy as jnp
        import numpy as np
        INT4_QMAX = 7.0

        def simulate_quantize_int4(w):
            scale = jnp.max(jnp.abs(w)) / INT4_QMAX
            q = jnp.clip(jnp.round(w / scale), -8.0, 7.0)
            return q * scale
        w = simulate_quantize_int4(kernel)
        y = jnp.einsum('bsd,df->bsf', x, w) + bias
        lora = jnp.einsum('bsr,rf->bsf', jnp.einsum('bsd,dr->bsr', x, a), b)
        return y + lora
    x = L0_attn_x
    xn = _layernorm(x, axis=-1)
    s = _L0_attn_ref(xn, L0_attn_Wq, L0_attn_bq, L0_attn_Wk, L0_attn_bk, L0_attn_Wv, L0_attn_bv, L0_attn_proj)
    g = _silu(_L0_ffn_ref(xn, L0_ffn_kernel, L0_ffn_bias, L0_ffn_a, L0_ffn_b))
    x = x + s * g
    return x

_drawn_inputs = setup_inputs


def setup_inputs(seed=0):
    import zlib

    import numpy as np

    out = dict(_drawn_inputs(seed))
    spreads = {}
    factors = {'L0_attn_Wq': 8.0,
     'L0_attn_bq': 8.0,
     'L0_attn_Wk': 8.0,
     'L0_attn_bk': 8.0,
     'L0_attn_Wv': 4.568,
     'L0_attn_bv': 4.16,
     'L0_attn_proj': 3.116,
     'L0_ffn_kernel': 3.774,
     'L0_ffn_bias': 8.0,
     'L0_ffn_a': 8.0,
     'L0_ffn_b': 8.0}
    for name, (base, spread) in spreads.items():
        noise = np.random.default_rng([zlib.crc32(name.encode()), seed]).standard_normal(out[name].shape)
        drawn = base * np.exp(spread * noise) if base else spread * noise
        out[name] = jnp.asarray(drawn.astype(out[name].dtype))
    for name, factor in factors.items():
        out[name] = (out[name] * factor).astype(out[name].dtype)
    return out
```

```python
import concourse.bass as bass
from concourse import mybir
from contextlib import ExitStack

F32 = mybir.dt.float32
F32R = mybir.dt.float32r
ALU = mybir.AluOpType
ACT = mybir.ActivationFunctionType
AX = mybir.AxisListType

P = 128
B, S, E = 4, 1024, 128
H, D = 16, 64
HP = H // 2
T = S // P
HALF = 4 * P
R = 16
EPS = 1e-5
SCALE = float(D) ** 0.5
QMAX, QMIN = 7.0, -8.0
ROUND = 1.5 * 2.0 ** 23
LOW = -3.0e38

PIECES = [[(0, 0, 4)], [(1, 1, 3), (3, 3, 1)], [(2, 2, 2)],
          [(0, 4, 4)], [(1, 4, 4)], [(2, 4, 4)], [(3, 4, 4)], [(4, 4, 4)], [(5, 5, 3), (7, 7, 1)], [(6, 6, 2)]]
NPC = len(PIECES)
FIRST_OF, LAST_OF = {0: 0, 1: 3}, {0: 2, 1: 9}
MASKED = [k for k in range(NPC) if any(j == s for j, s, _ in PIECES[k])]
MAXES = [(i, 0, P * (i + 1), True) for i in range(4)]
for _i in range(4, T):
    MAXES += [(_i, 0, HALF, False), (_i, HALF, P * (_i - 3), True)]
NMX = len(MAXES)
LAG = 2
SLOTS = 4


UNITS = B * HP
BODY = range(1, 1 + B)
LOOPS = (UNITS - 1) // B
REST = range(1 + B * LOOPS, UNITS)


def unit_items(u):
    items = []
    for k in range(2 * NPC):
        items.append(("score", u, k))
        if k >= LAG:
            items.append(("pv", u, k - LAG))
        elif u:
            items.append(("pv", u - 1, 2 * NPC + k - LAG))
        if k == 1:
            items.append(("maxT", u, 1))
        if k == 3 and u:
            items.append(("zT", u - 1, 1))
        if k == 6 and u:
            items.append(("proj", u - 1, 0))
        if k == 16:
            items.append(("zT", u, 0))
        if u % B == 0 and k == 9:
            items.append(("gate", u, 0))
        if u % B == 1 and k == 2:
            items.append(("gateT", u - 1, 0))
        if u + 1 < UNITS:
            if k < 4:
                items.append(("qk", u + 1, k))
            if k in (4, 5):
                items.append(("v", u + 1, k - 4))
            if 7 <= k < 19:
                items += [("max", u + 1, n) for n in range(2 * (k - 7), 2 * (k - 6))]
            if k == 14:
                items.append(("maxT", u + 1, 0))
        if u % B == 2 and u + 2 < UNITS and k in (8, 10):
            items.append(("w", u + 2, (k - 8) // 2))
    return items


PRE = [("w", 0, 0), ("w", 0, 1)] + [("qk", 0, n) for n in range(4)] + [("v", 0, 0), ("v", 0, 1)]
PRE += [("max", 0, n) for n in range(2 * NMX)] + [("maxT", 0, 0)]
TAIL = [("pv", UNITS - 1, 2 * NPC - 2), ("pv", UNITS - 1, 2 * NPC - 1), ("zT", UNITS - 1, 1), ("proj", UNITS - 1, 0)]

TURN_KINDS = ("qk", "v", "maxT", "zT", "proj", "w", "gate", "gateT")
TURNS = [x for x in PRE + [y for u in range(UNITS) for y in unit_items(u)] + TAIL if x[0] in TURN_KINDS]
LOOP_TURN = TURNS.index(next(x for x in unit_items(1) if x[0] in TURN_KINDS))
PERIOD = sum(x[0] in TURN_KINDS for u in BODY for x in unit_items(u))
assert PERIOD % 2 == 0
PER_PAIR = ("w", "gate", "gateT")


def attention_kernel(nc, x, Wq, bq, Wk, bk, Wv, bv, proj, kern, bias, lora_a, lora_b, out):
    x_t = x.rearrange("b (t p) e -> p (b t) e", p=P)
    w_rows = [w.rearrange("h d e -> (h d) e") for w in (Wq, Wk, Wv)]
    b_cols = [w.rearrange("h d -> d h") for w in (bq, bk)]
    bv_row = bv.rearrange("h d -> (h d)").rearrange("(a n) -> a n", a=1)

    ctx = ExitStack()
    with ctx:
        def sb(name, shape, dt=F32):
            return ctx.enter_context(nc.sbuf_tensor(name, shape, dt))

        x_sb = sb("x_sb", [P, B * T, E])
        xn = sb("xn", [P, B * T, E])
        gate_sb = sb("gate_sb", [P, B, E])
        out_sb = sb("out_sb", [P, 2, E])
        xT_hi = sb("xT_hi", [P, B * S], F32R)
        xT_lo = sb("xT_lo", [P, B * S], F32R)
        w_nat = sb("w_nat", [P, 3, E])
        wT_hi = sb("wT_hi", [P, 3 * P], F32R)
        wT_lo = sb("wT_lo", [P, 3 * P], F32R)
        b_all = sb("b_all", [D, 2, H])
        b_act = sb("b_act", [D, 2, 2])
        b_dve = sb("b_dve", [D, 2, 2])
        bv_all = sb("bv_all", [P, H * D])
        bv_cur = sb("bv_cur", [P, P])
        pj = sb("pj", [P, HP * E])
        QA = sb("QA", [P, 2, 2, S], F32R)
        KA = sb("KA", [P, 2, 2, S], F32R)
        QB = sb("QB", [D + 1, 2, 2, S], F32R)
        KB = sb("KB", [D + 1, 2, 2, S], F32R)
        V = sb("V", [P, 2, T, 2, D + 1])
        probs = sb("probs", [P, SLOTS, HALF])
        z = sb("z", [P, 4, 2, P])
        zT = sb("zT", [P, 8, 2, D])
        mx = sb("mx", [P, 2, 12])
        neg_max = sb("neg_max", [T, 2, P], F32R)
        rden = sb("rden", [P, 2, 4])
        causal = sb("causal", [P, HALF])
        ident = sb("ident", [P, P])
        gw_hi = sb("gw_hi", [P, P], F32R)
        gw_lo = sb("gw_lo", [P, P], F32R)
        g_bias = sb("g_bias", [P, 1])[:, :]
        g_exp = sb("g_exp", [P, HALF])
        g_den = sb("g_den", [P, HALF])
        gT = sb("gT", [P, HALF])
        stats = probs[:, 0, 0:B * T * 6].rearrange("p (t k) -> p t k", k=6)
        mv = probs[:, 1, 0:B * T * 2].rearrange("p (t k) -> p t k", k=2)
        kw = probs[:, 2, 0:P]
        kw_q = probs[:, 2, P:2 * P]
        kw_sum = probs[:, 2, 2 * P:3 * P]
        la = z[:, 0, 0, 0:R]
        laT = z[0:R, 0, 1, :]
        lb = z[0:R, 1, 0, :]
        kmax = z[:, 1, 1, 0:8]
        minus_half = z[:, 2, 0, 0:T]
        ones_row = z[0:1, 2, 1, :]
        kmax_row = z[0:1, 3, 0, 0:8]

        bank = [ctx.enter_context(nc.psum_tensor(f"bank{i}", [P, HALF], F32)) for i in range(8)]
        score_ps, max_ps, z_ps, turn_ps = bank[0:2], bank[2:4], bank[4:6], bank[6:8]

        count = {}

        def sem(name, per, span=1, weight=1, lead=0):
            count[name] = (ctx.enter_context(nc.semaphore(name)), per, span, weight, lead)
            return name

        scores_ready = sem("scores_ready", 2 * NPC)
        probs_used = sem("probs_used", 2 * NPC)
        maxes_ready = sem("maxes_ready", 2 * NMX)
        turns = dict(qk=4, v=2, maxT=2, zT=2, proj=1, w=2, gate=1, gateT=1)
        turn_ready = {k: sem(f"{k}_ready", n, span=B if k in PER_PAIR else 1) for k, n in turns.items()}
        probs_ready = sem("probs_ready", 2 * NPC)
        hi_ready = sem("hi_ready", 4 * 2)
        zT_copied = sem("zT_copied", 2)
        w_hi_ready = sem("w_hi_ready", 2, span=B)
        g_abs_ready = sem("g_abs_ready", 1, span=B)
        g_exp_ready = sem("g_exp_ready", 1, span=B)
        gate_stored = sem("gate_stored", 1, span=B)
        lo_ready = sem("lo_ready", 4)
        v_stored = sem("v_stored", 2)
        maxes_used = sem("maxes_used", 2 * NMX)
        mx_ready = sem("mx_ready", 2)
        neg_max_ready = sem("neg_max_ready", 2)
        rden_ready = sem("rden_ready", 4)
        z_stored = sem("z_stored", 4)
        gated = sem("gated", 1, lead=1)
        out_ready = sem("out_ready", 1)
        w_lo_ready = sem("w_lo_ready", 2, span=B)
        g_steps = sem("g_steps", 5, span=B)
        gT_ready = sem("gT_ready", 1, span=B)
        masked_ready = sem("masked_ready", 2 * len(MASKED))
        qA_filled = sem("qA_filled", 1, weight=16)
        kB_filled = sem("kB_filled", 1, weight=16)
        max_row = [sem(f"max_row{h}", 1, weight=16) for h in range(2)]
        w_loaded = sem("w_loaded", 3, span=B, weight=16)
        out_written = [sem(f"out_written{par}", 1, span=2, weight=16, lead=1) for par in range(2)]

        def inc(ins, name):
            ins.then_inc(count[name][0], count[name][3])

        def wait(eng, name, hp, u, n):
            s, per, span, weight, lead = count[name]
            fixed = (u // span * per + n + lead) * weight
            if isinstance(hp, int):
                assert hp == 0
                if fixed > 0:
                    eng.wait_ge(s, fixed)
            else:
                assert fixed > 0, (name, u, n)
                eng.wait_ge(s, hp * (B // span * per * weight) + fixed)

        def freed(turn):
            kind, u, n = turn
            name = {"qk": lo_ready, "v": v_stored, "maxT": neg_max_ready, "zT": zT_copied, "proj": gated,
                    "w": w_lo_ready, "gate": g_steps, "gateT": gate_stored}[kind]
            return name, u, n + 1

        def turn_bank(turn):
            return turn_ps[(TURNS.index(turn) - LOOP_TURN) % 2]

        def run(eng, item):
            for x in PRE + unit_items(0):
                item(0, *x)
            with eng.Fori(0, LOOPS) as hp:
                for u in BODY:
                    for x in unit_items(u):
                        item(hp, *x)
            for u in REST:
                for x in unit_items(u):
                    item(0, *x)
            for x in TAIL:
                item(0, *x)

        s_x = [ctx.enter_context(nc.semaphore(f"x_loaded{b}")) for b in range(B)]
        names = ("consts_loaded", "pj_loaded", "gw_loaded", "ident_zero", "ident_ready", "causal_ready", "ones_ready", "pow_ready", "var_eps_done",
                 "fixed_ready", "stats_done", "mv_done", "rstd_done", "xn_done", "xnT_ready", "xT_hi_ready",
                 "xT_lo_ready", "kmax_ready", "kmaxT_ready", "kmax_row_ready", "kmax_all_ready",
                 "laT_ready", "laT_copied", "ab_ready", "gw_step", "gw_ready", "max_seen", "probs_seen",)
        s = {n: ctx.enter_context(nc.semaphore(n)) for n in names}

        block = ctx.enter_context(nc.Block())

        @block.sync
        def _(sp):
            sp.dma_start(x_sb[:, 0:T, :], x_t[:, 0:T, :]).then_inc(s_x[0], 16)
            sp.dma_start(b_all[:, 0, :], b_cols[0], allow_slow_non_contiguous=True).then_inc(s["consts_loaded"], 16)
            sp.dma_start(b_all[:, 1, :], b_cols[1], allow_slow_non_contiguous=True).then_inc(s["consts_loaded"], 16)
            sp.dma_start(bv_all[:, :], bv_row.partition_broadcast(P)).then_inc(s["consts_loaded"], 16)
            for b in range(1, B):
                sp.dma_start(x_sb[:, b * T:(b + 1) * T, :], x_t[:, b * T:(b + 1) * T, :]).then_inc(s_x[b], 16)
            sp.dma_start(pj[:, :].rearrange("p (c e) -> p c e", e=E), proj.rearrange("(c p) e -> p c e", p=P)).then_inc(s["pj_loaded"], 16)

            def item(hp, kind, u, n):
                par = u % 2
                if (kind, n) == ("qk", 1):
                    wait(sp, hi_ready, hp, u, 4)
                    inc(sp.dma_start(QA[D:P, par, :, :].bitcast(F32), QA[0:D, par, :, :].bitcast(F32)), qA_filled)
                elif (kind, n) == ("qk", 3):
                    wait(sp, hi_ready, hp, u, 8)
                    inc(sp.dma_start(KB[0:D, par, :, :].bitcast(F32), KA[0:D, par, :, :].bitcast(F32)), kB_filled)
                elif kind == "maxT":
                    wait(sp, neg_max_ready, hp, u, n + 1)
                    inc(sp.dma_start(QB[D:D + 1, par, n, :].bitcast(F32), neg_max[:, n, :].bitcast(F32)), max_row[n])
                elif kind == "proj":
                    wait(sp, out_ready, hp, u, 1)
                    inc(sp.dma_start(out[u % B, bass.ds((hp + u // B) * P, P), :], out_sb[:, par, :]), out_written[par])

            for name in out_written:
                sp.sem_inc(count[name][0], 16)
            run(sp, item)
            for name in out_written:
                wait(sp, name, 0, UNITS, 0)

        @block.gpsimd
        def _(pool):
            def load_pair(pair):
                for i, w in enumerate(w_rows):
                    inc(pool.dma_start(w_nat[:, i, :], w[bass.ds(pair * P, P), :]), w_loaded)

            load_pair(0)
            pool.dma_start(kw, kern).then_inc(s["gw_loaded"], 16)
            pool.dma_start(la, lora_a).then_inc(s["gw_loaded"], 16)
            pool.dma_start(lb, lora_b).then_inc(s["gw_loaded"], 16)
            pool.dma_start(g_bias, bias.rearrange("(p a) -> p a", a=1)).then_inc(s["gw_loaded"], 16)
            pool.memset(minus_half, -0.5).then_inc(s["pow_ready"], 1)
            pool.memset(ident[:, :], 0.0).then_inc(s["ident_zero"], 1)
            pool.memset(causal[:, :], 0.0).then_inc(s["ident_zero"], 1)
            pool.wait_ge(s["ident_zero"], 2)
            pool.affine_select(out=ident[:, :], in_=ident[:, :], compare_op=ALU.not_equal, fill=1.0, base=0,
                               pattern=[[-1, P]], channel_multiplier=1).then_inc(s["ident_ready"], 1)
            pool.affine_select(out=causal[:, HALF - P:HALF], in_=causal[:, HALF - P:HALF], compare_op=ALU.is_ge,
                               fill=LOW, base=0, pattern=[[-1, P]], channel_multiplier=1).then_inc(s["causal_ready"], 1)
            pool.memset(ones_row, 1.0).then_inc(s["ones_ready"], 1)
            for par in range(2):
                pool.memset(V[:, par, :, :, D:D + 1], SCALE).then_inc(s["fixed_ready"], 1)
            pool.wait_ge(s["pow_ready"], 1)
            for b in range(B):
                var = mv[:, b * T:(b + 1) * T, 1]
                pool.wait_ge(s["var_eps_done"], b + 1)
                pool.tensor_tensor(out=var, in0=var, in1=minus_half, op=ALU.pow).then_inc(s["rstd_done"], 1)

            def item(hp, kind, u, n):
                if kind == "w" and n == 1:
                    wait(pool, turn_ready["w"], hp, u, 2)
                    load_pair((hp + u // B + 1) % HP)
                elif kind == "score" and n % NPC in MASKED:
                    segments = PIECES[n % NPC]
                    slot = probs[:, n % SLOTS, :].rearrange("p (t n) -> p t n", n=P)
                    diag = slot[:, 0::3, :] if len(segments) == 2 else slot[:, 0:1, :]
                    wait(pool, probs_ready, hp, u, n + 1)
                    pool.sem_inc(s["probs_seen"], 1)
                    inc(pool.affine_select(out=diag, in_=diag, compare_op=ALU.is_ge, fill=0.0, base=0,
                                           pattern=[[0, len(segments)], [1, P]], channel_multiplier=-1), masked_ready)

            run(pool, item)
            wait(pool, w_loaded, 0, UNITS, 3)

        @block.scalar
        def _(act):
            for n in range(2 * B):
                act.wait_ge(s["xnT_ready"], n + 1)
                nc.scalar.activation(xT_hi[:, n * HALF:(n + 1) * HALF], bank[n][:, :], ACT.Copy
                                     ).then_inc(s["xT_hi_ready"], 1)
            act.wait_ge(s["consts_loaded"], 48)
            act.wait_ge(s["gw_loaded"], 64)

            def item(hp, kind, u, n):
                turn, par = (kind, u, n), u % 2
                if kind == "score":
                    wait(act, scores_ready, hp, u, n + 1)
                    wait(act, probs_used, hp, u, n + 1 - SLOTS)
                    cols = P * sum(w for _, _, w in PIECES[n % NPC])
                    inc(nc.scalar.activation(probs[:, n % SLOTS, 0:cols], score_ps[n % 2][:, 0:cols], ACT.Exp,
                                             scale=1.0 / SCALE), probs_ready)
                elif kind == "qk":
                    which, half = n // 2, n % 2
                    wait(act, turn_ready[kind], hp, u, n + 1)
                    if u % B == 0 and n == 0:
                        wait(act, w_hi_ready, hp, u, 2)
                    for h in range(2):
                        dst = (QA, KA)[which][0:D, par, h, half * HALF:(half + 1) * HALF]
                        inc(nc.scalar.activation(dst, turn_bank(turn)[h * D:(h + 1) * D, :], ACT.Identity,
                                                 bias=b_act[:, which, h:h + 1]), hi_ready)
                elif kind == "zT":
                    wait(act, turn_ready[kind], hp, u, n + 1)
                    if n == 0:
                        wait(act, turn_ready["proj"], hp, u, 0)
                    for tp in range(2):
                        row = (2 * n + tp) * 16
                        src = turn_bank(turn)[:, tp * 2 * P:(tp + 1) * 2 * P].rearrange("p (h a c) -> p c h a", h=2, c=8)
                        ins = nc.scalar.copy(zT[:, :, :, row:row + 16], src)
                    inc(ins, zT_copied)
                elif kind == "w":
                    wait(act, turn_ready[kind], hp, u, n + 1)
                    cols = slice(0, 2 * P) if n == 0 else slice(2 * P, 3 * P)
                    if n == 0:
                        wait(act, hi_ready, hp, u, 0)
                        nc.scalar.copy(b_act[:, :, :], b_all[:, :, bass.ds((hp + u // B) * 2, 2)])
                    inc(nc.scalar.activation(wT_hi[:, cols], turn_bank(turn)[:, 0:cols.stop - cols.start], ACT.Copy),
                        w_hi_ready)
                elif kind == "gate":
                    wait(act, turn_ready[kind], hp, u, 1)
                    wait(act, gT_ready, hp, u, 0)
                    inc(nc.scalar.activation(g_exp[:, :], turn_bank(turn)[:, :], ACT.Abs, bias=g_bias), g_abs_ready)
                    wait(act, g_abs_ready, hp, u, 1)
                    inc(nc.scalar.activation(g_exp[:, :], g_exp[:, :], ACT.Exp, scale=-1.0), g_exp_ready)
                elif kind == "gateT":
                    wait(act, turn_ready[kind], hp, u, 1)
                    wait(act, gated, hp, u, 0)
                    inc(nc.scalar.copy(gate_sb[:, :, :], turn_bank(turn)[:, :].rearrange("p (t e) -> p t e", t=4)),
                        gate_stored)

            run(act, item)

        @block.vector
        def _(dve):
            dve.sem_inc(count[gated][0], 1)
            for b in range(B):
                dve.wait_ge(s_x[b], 16)
                for t in range(b * T, (b + 1) * T):
                    nc.vector.bn_stats(stats[:, t, :], x_sb[:, t, :]).then_inc(s["stats_done"], 1)
                for t in range(b * T, (b + 1) * T):
                    dve.wait_ge(s["stats_done"], t + 1)
                    nc.vector.bn_aggr(mv[:, t, :], stats[:, t, :]).then_inc(s["mv_done"], 1)
                dve.wait_ge(s["mv_done"], (b + 1) * T)
                nc.vector.tensor_scalar(mv[:, b * T:(b + 1) * T, 1], mv[:, b * T:(b + 1) * T, 1], EPS, None,
                                        ALU.add).then_inc(s["var_eps_done"], 1)
                dve.wait_ge(s["rstd_done"], b + 1)
                for t in range(b * T, (b + 1) * T):
                    nc.vector.tensor_scalar(xn[:, t, :], x_sb[:, t, :], mv[:, t, 0:1], mv[:, t, 1:2],
                                            ALU.subtract, ALU.mult).then_inc(s["xn_done"], 1)
            for n in range(2 * B):
                cols = slice(n * HALF, (n + 1) * HALF)
                dve.wait_ge(s["xT_hi_ready"], n + 1)
                nc.vector.tensor_tensor(out=xT_lo[:, cols], in0=bank[n][:, :], in1=xT_hi[:, cols].bitcast(F32),
                                        op=ALU.subtract).then_inc(s["xT_lo_ready"], 1)
            step = [0]

            def then(ins):
                step[0] += 1
                ins.then_inc(s["gw_step"], 1)
                dve.wait_ge(s["gw_step"], step[0])

            dve.wait_ge(s["gw_loaded"], 64)
            nc.vector.tensor_reduce(kmax[:, 0:1], kw, AX.X, ALU.max, apply_absolute_value=True
                                    ).then_inc(s["kmax_ready"], 1)
            dve.wait_ge(s["kmaxT_ready"], 1)
            nc.vector.reduce_max(kmax_row[0:1, 0:1], bank[0][0:1, 0:P], AX.X).then_inc(s["kmax_row_ready"], 1)
            dve.wait_ge(s["laT_ready"], 1)
            nc.vector.tensor_copy(laT, bank[2][0:R, 0:P]).then_inc(s["laT_copied"], 1)
            dve.wait_ge(s["kmax_all_ready"], 1)
            then(nc.vector.tensor_scalar(kmax[:, 1:2], bank[1][:, 0:1], 1.0 / QMAX, None, ALU.mult))
            then(nc.vector.reciprocal(kmax[:, 2:3], kmax[:, 1:2]))
            then(nc.vector.tensor_scalar(kw_q, kw, kmax[:, 2:3], None, ALU.mult))
            then(nc.vector.tensor_scalar(kw_q, kw_q, ROUND, -ROUND, ALU.add, ALU.add))
            then(nc.vector.tensor_scalar(kw_q, kw_q, QMIN, QMAX, ALU.max, ALU.min))
            dve.wait_ge(s["ab_ready"], 1)
            then(nc.vector.scalar_tensor_tensor(out=kw_sum, in0=kw_q, scalar=kmax[:, 1:2], in1=bank[3][:, 0:P],
                                                op0=ALU.mult, op1=ALU.add))
            then(nc.vector.tensor_copy(gw_hi[:, :], kw_sum))
            nc.vector.tensor_tensor(out=gw_lo[:, :], in0=kw_sum, in1=gw_hi[:, :].bitcast(F32), op=ALU.subtract
                                    ).then_inc(s["gw_ready"], 1)
            for par in range(2):
                nc.vector.memset(KB[D:D + 1, par, :, :].bitcast(F32), 1.0).then_inc(s["fixed_ready"], 1)
            dve.wait_ge(s["causal_ready"], 1)
            dve.wait_ge(s["fixed_ready"], 4)

            def row_max(hp, u, n):
                h, (i, _, keys, diagonal) = n // NMX, MAXES[n % NMX]
                col = i if diagonal else T + i - 4
                ps = max_ps[n % 2][:, 0:keys]
                if n % NMX == 0:
                    wait(dve, turn_ready["maxT"], hp, u, h + 1 - 2)
                wait(dve, maxes_ready, hp, u, n + 1)
                if diagonal:
                    dve.sem_inc(s["max_seen"], 1)
                    ins = nc.vector.tensor_tensor_reduce(out=ps, in0=ps, in1=causal[:, HALF - keys:HALF], scale=1.0,
                                                         scalar=LOW, op0=ALU.add, op1=ALU.max,
                                                         accum_out=mx[:, h, col:col + 1])
                else:
                    ins = nc.vector.reduce_max(mx[:, h, col:col + 1], ps, AX.X)
                inc(ins, maxes_used)
                if n % NMX == NMX - 1:
                    wait(dve, maxes_used, hp, u, n + 1)
                    inc(nc.vector.tensor_tensor(out=mx[:, h, 4:8], in0=mx[:, h, 4:8], in1=mx[:, h, 8:12], op=ALU.max),
                        mx_ready)

            def store_z(hp, u, h, half):
                ps = z_ps[half][:, 0:4 * (D + 1)].rearrange("p (t c) -> p t c", t=4)
                n = h * 2 + half + 1
                wait(dve, probs_used, hp, u, h * NPC + LAST_OF[half] + 1)
                inc(nc.vector.reciprocal(rden[:, half, :], ps[:, :, D]), rden_ready)
                if h == 0:
                    wait(dve, turn_ready["zT"], hp, u, half + 1 - 2)
                wait(dve, rden_ready, hp, u, n)
                for tp in range(2):
                    ins = nc.vector.tensor_tensor(
                        out=z[:, 2 * half + tp, h, :].rearrange("p (c d) -> p c d", c=2),
                        in0=ps[:, 2 * tp:2 * tp + 2, 0:D],
                        in1=rden[:, half, 2 * tp:2 * tp + 2].unsqueeze(2).to_broadcast([P, 2, D]), op=ALU.mult)
                inc(ins, z_stored)

            def item(hp, kind, u, n):
                turn, par = (kind, u, n), u % 2
                if kind == "pv" and n % NPC in (LAST_OF[0], LAST_OF[1]):
                    store_z(hp, u, n // NPC, int(n % NPC == LAST_OF[1]))
                elif kind == "max":
                    row_max(hp, u, n)
                elif kind == "qk":
                    which, half = n // 2, n % 2
                    cols = slice(half * HALF, (half + 1) * HALF)
                    wait(dve, hi_ready, hp, u, 2 * (n + 1))
                    if u % B == 0 and n == 0:
                        wait(dve, w_lo_ready, hp, u, 2)
                    for h in range(2):
                        hi = (QA, KA)[which][0:D, par, h, cols]
                        lo = (QB[0:D, par, h, cols], KA[D:P, par, h, cols])[which]
                        ins = nc.vector.scalar_tensor_tensor(out=lo, in0=turn_bank(turn)[h * D:(h + 1) * D, :],
                                                             scalar=b_dve[:, which, h:h + 1], in1=hi.bitcast(F32),
                                                             op0=ALU.add, op1=ALU.subtract)
                    inc(ins, lo_ready)
                elif kind == "v":
                    wait(dve, turn_ready[kind], hp, u, n + 1)
                    dst = V[:, par, 4 * n:4 * n + 4, :, 0:D]
                    inc(nc.vector.tensor_tensor(
                        out=dst, in0=turn_bank(turn)[:, :].rearrange("p (t h d) -> p t h d", t=4, h=2),
                        in1=bv_cur[:, :].rearrange("p (h d) -> p h d", h=2).unsqueeze(1).to_broadcast([P, 4, 2, D]),
                        op=ALU.add), v_stored)
                elif kind == "maxT":
                    wait(dve, turn_ready[kind], hp, u, n + 1)
                    wait(dve, max_row[n], hp, u, 0)
                    inc(nc.vector.tensor_scalar(neg_max[:, n, :], turn_bank(turn)[0:T, 0:P], -1.0, None, ALU.mult),
                        neg_max_ready)
                elif kind == "proj":
                    wait(dve, turn_ready[kind], hp, u, 1)
                    wait(dve, gate_stored, hp, u, 1)
                    wait(dve, out_written[par], hp, u, 0)
                    inc(nc.vector.tensor_tensor(out=out_sb[:, par, :], in0=turn_bank(turn)[:, 0:E],
                                                in1=gate_sb[:, u % B, :], op=ALU.mult), gated)
                    wait(dve, gated, hp, u, 1)
                    inc(nc.vector.tensor_tensor(out=out_sb[:, par, :], in0=out_sb[:, par, :],
                                                in1=x_sb[:, bass.ds(u % B * T + hp + u // B, 1), :], op=ALU.add),
                        out_ready)
                elif kind == "w":
                    cols = slice(0, 2 * P) if n == 0 else slice(2 * P, 3 * P)
                    pair = hp + u // B
                    if n == 0:
                        wait(dve, v_stored, hp, u - 1, 2)
                        nc.vector.tensor_copy(b_dve[:, :, :], b_all[:, :, bass.ds(pair * 2, 2)])
                        nc.vector.tensor_copy(bv_cur[:, :], bv_all[:, bass.ds(pair * P, P)])
                    wait(dve, w_hi_ready, hp, u, n + 1)
                    inc(nc.vector.tensor_tensor(out=wT_lo[:, cols], in0=turn_bank(turn)[:, 0:cols.stop - cols.start],
                                                in1=wT_hi[:, cols].bitcast(F32), op=ALU.subtract), w_lo_ready)
                elif kind == "gate":
                    wait(dve, g_exp_ready, hp, u, 1)
                    wait(dve, turn_ready["gateT"], hp, u, 0)
                    inc(nc.vector.tensor_scalar(gT[:, :], turn_bank(turn)[:, :], g_bias, None, ALU.add), g_steps)
                    inc(nc.vector.tensor_scalar(g_den[:, :], g_exp[:, :], 1.0, None, ALU.add), g_steps)
                    wait(dve, g_steps, hp, u, 2)
                    inc(nc.vector.scalar_tensor_tensor(out=g_exp[:, :], in0=gT[:, :], scalar=0.0, in1=g_exp[:, :],
                                                       op0=ALU.is_ge, op1=ALU.max), g_steps)
                    inc(nc.vector.reciprocal(g_den[:, :], g_den[:, :]), g_steps)
                    wait(dve, g_steps, hp, u, 4)
                    inc(nc.vector.tensor_tensor(out=gT[:, :], in0=gT[:, :], in1=g_exp[:, :], op=ALU.mult), g_steps)
                    wait(dve, g_steps, hp, u, 5)
                    inc(nc.vector.tensor_tensor(out=gT[:, :], in0=gT[:, :], in1=g_den[:, :], op=ALU.mult), gT_ready)

            dve.wait_ge(s["consts_loaded"], 48)
            run(dve, item)

        @block.tensor
        def _(pe):
            mm = nc.tensor.matmul
            pe.wait_ge(s["ident_ready"], 1)
            for n in range(2 * B):
                pe.wait_ge(s["xn_done"], (n + 1) * 4)
                for i in range(4):
                    last = nc.tensor.transpose(bank[n][:, i * P:(i + 1) * P], xn[:, n * 4 + i, :], ident[:, :])
                last.then_inc(s["xnT_ready"], 1)
            pe.wait_ge(s["xT_lo_ready"], 1)
            pe.wait_ge(s["kmax_ready"], 1)
            nc.tensor.transpose(bank[0][0:1, 0:P], kmax[:, 0:1], ident[:, :]).then_inc(s["kmaxT_ready"], 1)
            pe.wait_ge(s["xT_lo_ready"], 3)
            nc.tensor.transpose(bank[2][0:R, 0:P], la, ident[:, :]).then_inc(s["laT_ready"], 1)
            pe.wait_ge(s["kmax_row_ready"], 1)
            pe.wait_ge(s["ones_ready"], 1)
            mm(bank[1][:, 0:1], ones_row, kmax_row[0:1, 0:1], start=True, stop=True).then_inc(s["kmax_all_ready"], 1)
            pe.wait_ge(s["laT_copied"], 1)
            pe.wait_ge(s["xT_lo_ready"], 4)
            mm(bank[3][:, 0:P], laT, lb, start=True, stop=True).then_inc(s["ab_ready"], 1)
            pe.wait_ge(s["xT_lo_ready"], 2 * B)
            pe.wait_ge(s["gw_ready"], 1)
            pe.wait_ge(s["fixed_ready"], 4)
            pe.wait_ge(s["pj_loaded"], 16)

            def three(out, w_hi, w_lo, m_hi, m_lo, **kw):
                mm(out, w_hi, m_hi, start=True, stop=False, **kw)
                mm(out, w_hi, m_lo, start=False, stop=False, **kw)
                return mm(out, w_lo, m_hi, start=False, stop=True, **kw)

            def item(hp, kind, u, n):
                turn, b, par = (kind, u, n), u % B, u % 2
                if kind == "score":
                    h, k = n // NPC, n % NPC
                    ps = score_ps[n % 2]
                    if k == 0:
                        wait(pe, max_row[h], hp, u, 1)
                        if h == 0:
                            wait(pe, kB_filled, hp, u, 1)
                    wait(pe, probs_ready, hp, u, n + 1 - 2)
                    at = 0
                    for j, s0, w in PIECES[k]:
                        keys, queries = slice(j * P, (j + 1) * P), slice(s0 * P, (s0 + w) * P)
                        dst = ps[:, at:at + w * P]
                        mm(dst, KA[:, par, h, keys], QA[:, par, h, queries], start=True, stop=False)
                        last = mm(dst, KB[:, par, h, keys], QB[:, par, h, queries], start=False, stop=True)
                        at += w * P
                    inc(last, scores_ready)
                elif kind == "pv":
                    h, k = n // NPC, n % NPC
                    half = int(k >= FIRST_OF[1])
                    first = k == FIRST_OF[half]
                    if n == 0:
                        wait(pe, v_stored, hp, u, 2)
                    if first:
                        wait(pe, z_stored, hp, u, h * 2 + half + 1 - 2)
                    if k in MASKED:
                        wait(pe, masked_ready, hp, u, h * len(MASKED) + MASKED.index(k) + 1)
                    else:
                        wait(pe, probs_ready, hp, u, n + 1)
                    at = 0
                    for j, s0, w in PIECES[k]:
                        i = s0
                        while i < s0 + w:
                            alone = i % 2
                            width = (1 if alone else 2) * P
                            for odd in range(2):
                                c = (i // 2 % 2 * 2 + odd) * (D + 1)
                                dst = z_ps[half][D if alone else 0:P, c:c + D + 1]
                                last = mm(dst, probs[:, n % SLOTS, at + odd:at + width:2], V[:, par, j, h, :],
                                          start=first, stop=j == i or j == i + 1, skip_group_check=True)
                                first = False
                            at += width
                            i += 1 if alone else 2
                    inc(last, probs_used)
                elif kind == "max":
                    h, (i, key0, keys, _) = n // NMX, MAXES[n % NMX]
                    if n == 0:
                        wait(pe, lo_ready, hp, u, 4)
                        wait(pe, qA_filled, hp, u, 1)
                    wait(pe, maxes_used, hp, u, n + 1 - 2)
                    inc(mm(max_ps[n % 2][:, 0:keys], QA[:, par, h, i * P:(i + 1) * P],
                           KA[:, par, h, key0:key0 + keys], start=True, stop=True), maxes_ready)
                else:
                    if TURNS.index(turn) >= 2:
                        name, before, at = freed(TURNS[TURNS.index(turn) - 2])
                        wait(pe, name, hp, before, at)
                    ps = turn_bank(turn)
                    if kind == "qk":
                        which, half = n // 2, n % 2
                        if b == 0 and n == 0:
                            wait(pe, w_lo_ready, hp, u, 2)
                        col0 = b * S + half * HALF
                        w = slice(which * P, (which + 1) * P)
                        last = three(ps[:, :], wT_hi[:, w], wT_lo[:, w], xT_hi[:, col0:col0 + HALF],
                                     xT_lo[:, col0:col0 + HALF])
                    elif kind == "v":
                        for i in range(4):
                            tok = b * S + (4 * n + i) * P
                            last = three(ps[:, i * P:(i + 1) * P], xT_hi[:, tok:tok + P], xT_lo[:, tok:tok + P],
                                         wT_hi[:, 2 * P:3 * P], wT_lo[:, 2 * P:3 * P])
                    elif kind == "maxT":
                        wait(pe, mx_ready, hp, u, n + 1)
                        last = nc.tensor.transpose(ps[0:T, 0:P], mx[:, n, 0:T], ident[:, :])
                    elif kind == "zT":
                        wait(pe, z_stored, hp, u, 2 + n + 1)
                        for tp in range(2):
                            for h in range(2):
                                c = (tp * 2 + h) * P
                                last = nc.tensor.transpose(ps[:, c:c + P], z[:, 2 * n + tp, h, :], ident[:, :])
                    elif kind == "proj":
                        wait(pe, zT_copied, hp, u, 2)
                        for c in range(8):
                            last = mm(ps[:, 0:E], zT[:, c, :, :].rearrange("p h a -> p (h a)"),
                                      pj[:, c * E:(c + 1) * E], start=c == 0, stop=c == 7)
                    elif kind == "w":
                        if n == 0:
                            wait(pe, w_loaded, hp, u, 3)
                        for i in (0, 1) if n == 0 else (2,):
                            c = (i % 2) * P
                            last = nc.tensor.transpose(ps[:, c:c + P], w_nat[:, i, :], ident[:, :])
                    elif kind == "gate":
                        rows = bass.ds((hp + u // B) * P, P)
                        last = three(ps[:, :], gw_hi[:, :], gw_lo[:, :],
                                     xT_hi[:, :].rearrange("p (b s) -> p b s", b=B)[:, :, rows],
                                     xT_lo[:, :].rearrange("p (b s) -> p b s", b=B)[:, :, rows])
                    elif kind == "gateT":
                        wait(pe, gT_ready, hp, u, 1)
                        for i in range(4):
                            last = nc.tensor.transpose(ps[:, i * P:(i + 1) * P], gT[:, i * P:(i + 1) * P], ident[:, :])
                    inc(last, turn_ready[kind])

            run(pe, item)


_INS = ["L0_attn_x", "L0_attn_Wq", "L0_attn_bq", "L0_attn_Wk", "L0_attn_bk", "L0_attn_Wv", "L0_attn_bv",
        "L0_attn_proj", "L0_ffn_kernel", "L0_ffn_bias", "L0_ffn_a", "L0_ffn_b"]


def kernel(**inputs):
    import numpy as _np
    import concourse.bacc as _bacc
    from concourse import mybir as _mybir
    from concourse.bass_utils import run_bass_kernel_spmd as _run

    nc = _bacc.Bacc("TRN2", target_bir_lowering=False, num_devices=1)
    arrays, args = {}, []
    for name in _INS:
        a = _np.ascontiguousarray(inputs[name])
        arrays[f"in_{name}_dram"] = a
        args.append(nc.dram_tensor(f"in_{name}_dram", a.shape, _mybir.dt.from_np(a.dtype), kind="ExternalInput").ap())
    args.append(nc.dram_tensor("out_dram", (B, S, E), _mybir.dt.float32, kind="ExternalOutput").ap())
    attention_kernel(nc, *args)
    r = _run(nc, [arrays], core_ids=[0])
    return r.results[0]["out_dram"]
```

```python
import concourse.bass as bass
from concourse import mybir
from contextlib import ExitStack

F32 = mybir.dt.float32
F32R = mybir.dt.float32r
ALU = mybir.AluOpType
ACT = mybir.ActivationFunctionType
AX = mybir.AxisListType

P = 128
B, S, E = 4, 1024, 128
H, D = 16, 64
HP = H // 2
T = S // P
HALF = 4 * P
R = 16
EPS = 1e-5
SCALE = float(D) ** 0.5
QMAX, QMIN = 7.0, -8.0
ROUND = 1.5 * 2.0 ** 23
LOW = -3.0e38

PIECES = [[(0, 0, 4)], [(1, 1, 3), (3, 3, 1)], [(2, 2, 2)],
          [(0, 4, 4)], [(1, 4, 4)], [(2, 4, 4)], [(3, 4, 4)], [(4, 4, 4)], [(5, 5, 3), (7, 7, 1)], [(6, 6, 2)]]
NPC = len(PIECES)
FIRST_OF, LAST_OF = {0: 0, 1: 3}, {0: 2, 1: 9}
MASKED = [k for k in range(NPC) if any(j == s for j, s, _ in PIECES[k])]
MAXES = [(i, 0, P * (i + 1), True) for i in range(4)]
for _i in range(4, T):
    MAXES += [(_i, 0, HALF, False), (_i, HALF, P * (_i - 3), True)]
NMX = len(MAXES)
LAG = 2
SLOTS = 4


UNITS = B * HP
BODY = range(1, 1 + B)
LOOPS = (UNITS - 1) // B
REST = range(1 + B * LOOPS, UNITS)


SILU_AT = (14, 15, 17)
QK_AT = (0, 3, 5, 7)


def unit_items(u):
    items = []
    for k in range(2 * NPC):
        items.append(("score", u, k))
        if u + 1 < UNITS and k >= 8:
            items.append(("max", u + 1, 2 * (k - 8)))
        if k >= LAG:
            items.append(("pv", u, k - LAG))
        elif u:
            items.append(("pv", u - 1, 2 * NPC + k - LAG))
        if k == 1:
            items.append(("maxT", u, 1))
        if k == 4 and u:
            items.append(("zT", u - 1, 1))
        if k == 6 and u:
            items.append(("proj", u - 1, 0))
        if u == 0:
            items += FIRST_UNIT.get(k, [])
        if k == 12:
            items.append(("gate", u, 0))
        if k in SILU_AT:
            items.append(("silu", u, SILU_AT.index(k)))
        if k == 19:
            items.append(("gateT", u, 0))
        if k == 18:
            items.append(("zT", u, 0))
        if u + 1 < UNITS:
            if k in QK_AT:
                items.append(("qk", u + 1, QK_AT.index(k)))
            if k in (8, 9):
                items.append(("v", u + 1, k - 8))
            if k >= 8:
                items.append(("max", u + 1, 2 * (k - 8) + 1))
            if k == 16:
                items.append(("maxT", u + 1, 0))
        if u % B == 2 and u + 2 < UNITS and k in (9, 11):
            items.append(("w", u + 2, (k - 9) // 2))
    return items


PRE = [("stats", 0, 0), ("w", 0, 0), ("w", 0, 1), ("norm", 0, 0), ("stats", 0, 1), ("xT", 0, 0), ("xT", 0, 1)]
PRE += [("qk", 0, n) for n in range(4)] + [("v", 0, 0), ("v", 0, 1)]
PRE += [("max", 0, n) for n in range(NMX)] + [("maxT", 0, 0)]
PRE += [("norm", 0, 1), ("xT", 0, 2), ("xT", 0, 3)] + [("max", 0, n) for n in range(NMX, 2 * NMX)]
FIRST_UNIT = {2: [("stats", 0, 2)], 3: [("norm", 0, 2)], 5: [("xT", 0, 4)], 7: [("xT", 0, 5)],
              8: [("stats", 0, 3), ("gk", 0, 0)], 9: [("norm", 0, 3), ("gk", 0, 1)], 10: [("gk", 0, 2), ("xT", 0, 6)],
              11: [("gk", 0, 3), ("xT", 0, 7)]}
TAIL = [("pv", UNITS - 1, 2 * NPC - 2), ("pv", UNITS - 1, 2 * NPC - 1), ("zT", UNITS - 1, 1), ("proj", UNITS - 1, 0)]

TURN_KINDS = ("qk", "v", "maxT", "zT", "proj", "w", "gate", "gateT", "xT", "gk")
TURNS = [x for x in PRE + [y for u in range(UNITS) for y in unit_items(u)] + TAIL if x[0] in TURN_KINDS]
LOOP_TURN = TURNS.index(next(x for x in unit_items(1) if x[0] in TURN_KINDS))
PERIOD = sum(x[0] in TURN_KINDS for u in BODY for x in unit_items(u))
assert PERIOD % 2 == 0
PER_PAIR = ("w",)


def attention_kernel(nc, x, Wq, bq, Wk, bk, Wv, bv, proj, kern, bias, lora_a, lora_b, out):
    x_t = x.rearrange("b (t p) e -> p (b t) e", p=P)
    w_rows = [w.rearrange("h d e -> (h d) e") for w in (Wq, Wk, Wv)]
    b_cols = [w.rearrange("h d -> d h") for w in (bq, bk)]
    bv_row = bv.rearrange("h d -> (h d)").rearrange("(a n) -> a n", a=1)

    ctx = ExitStack()
    with ctx:
        def sb(name, shape, dt=F32):
            return ctx.enter_context(nc.sbuf_tensor(name, shape, dt))

        x_sb = sb("x_sb", [P, B * T, E])
        xn = sb("xn", [P, B * T, E])
        gate_sb = sb("gate_sb", [P, E])
        out_sb = sb("out_sb", [P, 2, E])
        xT_hi = sb("xT_hi", [P, B * S], F32R)
        xT_lo = sb("xT_lo", [P, B * S], F32R)
        w_nat = sb("w_nat", [P, 3, E])
        wT_hi = sb("wT_hi", [P, 3 * P], F32R)
        wT_lo = sb("wT_lo", [P, 3 * P], F32R)
        b_all = sb("b_all", [D, 2, H])
        b_act = sb("b_act", [D, 2, 2])
        b_dve = sb("b_dve", [D, 2, 2])
        bv_all = sb("bv_all", [P, H * D])
        bv_cur = sb("bv_cur", [P, P])
        pj = sb("pj", [P, HP * E])
        QA = sb("QA", [P, 2, 2, S], F32R)
        KA = sb("KA", [P, 2, 2, S], F32R)
        QB = sb("QB", [D + 1, 2, 2, S], F32R)
        KB = sb("KB", [D + 1, 2, 2, S], F32R)
        V = sb("V", [P, 2, T, 2, D + 1])
        probs = sb("probs", [P, SLOTS, HALF])
        z = sb("z", [P, 4, 2, P])
        zT = sb("zT", [P, 8, 2, D])
        mx = sb("mx", [P, 2, 12])
        neg_max = sb("neg_max", [T, 2, P], F32R)
        rden = sb("rden", [P, 2, 4])
        causal = sb("causal", [P, HALF])
        ident = sb("ident", [P, P])
        gw_hi = sb("gw_hi", [P, P], F32R)
        gw_lo = sb("gw_lo", [P, P], F32R)
        g_bias = sb("g_bias", [P, 1])[:, :]
        g_exp = sb("g_exp", [P, P])
        g_den = sb("g_den", [P, P])
        gT = sb("gT", [P, P])
        stats = sb("stats", [P, B * T, 6])
        mv = sb("mv", [P, B * T, 2])
        kw = sb("kw", [P, P])[:, :]
        kw_q = sb("kw_q", [P, P])[:, :]
        kw_sum = sb("kw_sum", [P, P])[:, :]
        la = sb("la", [P, R])[:, :]
        laT = sb("laT", [R, P])[:, :]
        lb = sb("lb", [R, P])[:, :]
        kmax = sb("kmax", [P, 8])[:, :]
        minus_half = sb("minus_half", [P, T])[:, :]
        ones_row = sb("ones_row", [1, P])[:, :]
        kmax_row = sb("kmax_row", [1, 8])[:, :]

        bank = [ctx.enter_context(nc.psum_tensor(f"bank{i}", [P, HALF], F32)) for i in range(8)]
        score_ps, max_ps, z_ps, turn_ps = bank[0:2], bank[2:4], bank[4:6], bank[6:8]

        count = {}

        def sem(name, per, span=1, weight=1, lead=0):
            count[name] = (ctx.enter_context(nc.semaphore(name)), per, span, weight, lead)
            return name

        scores_ready = sem("scores_ready", 2 * NPC)
        probs_used = sem("probs_used", 2 * NPC)
        maxes_ready = sem("maxes_ready", 2 * NMX)
        turns = dict(qk=4, v=2, maxT=2, zT=2, proj=1, w=2, gate=1, gateT=1, xT=2 * B, gk=4)
        turn_ready = {k: sem(f"{k}_ready", n, span=B if k in PER_PAIR else 1) for k, n in turns.items()}
        probs_ready = sem("probs_ready", 2 * NPC)
        hi_ready = sem("hi_ready", 4 * 2)
        zT_copied = sem("zT_copied", 2)
        w_hi_ready = sem("w_hi_ready", 2, span=B)
        xT_hi_ready = sem("xT_hi_ready", 2 * B)
        g_abs_ready = sem("g_abs_ready", 1)
        g_exp_ready = sem("g_exp_ready", 1)
        gate_stored = sem("gate_stored", 1)
        lo_ready = sem("lo_ready", 4)
        v_stored = sem("v_stored", 2)
        maxes_used = sem("maxes_used", 2 * NMX)
        mx_ready = sem("mx_ready", 2)
        neg_max_ready = sem("neg_max_ready", 2)
        rden_ready = sem("rden_ready", 4)
        z_stored = sem("z_stored", 4)
        gated = sem("gated", 1, lead=1)
        out_ready = sem("out_ready", 1)
        w_lo_ready = sem("w_lo_ready", 2, span=B)
        xT_lo_ready = sem("xT_lo_ready", 2 * B)
        gk_used = sem("gk_used", 4)
        g_steps = sem("g_steps", 5)
        gT_ready = sem("gT_ready", 1)
        masked_ready = sem("masked_ready", 2 * len(MASKED))
        qA_filled = sem("qA_filled", 1, weight=16)
        kB_filled = sem("kB_filled", 1, weight=16)
        max_row = [sem(f"max_row{h}", 1, weight=16) for h in range(2)]
        w_loaded = sem("w_loaded", 3, span=B, weight=16)
        out_written = [sem(f"out_written{par}", 1, span=2, weight=16, lead=1) for par in range(2)]

        def inc(ins, name):
            ins.then_inc(count[name][0], count[name][3])

        def wait(eng, name, hp, u, n):
            s, per, span, weight, lead = count[name]
            fixed = (u // span * per + n + lead) * weight
            if isinstance(hp, int):
                assert hp == 0
                if fixed > 0:
                    eng.wait_ge(s, fixed)
            else:
                assert fixed > 0, (name, u, n)
                eng.wait_ge(s, hp * (B // span * per * weight) + fixed)

        def freed(turn):
            kind, u, n = turn
            name = {"qk": lo_ready, "v": v_stored, "maxT": neg_max_ready, "zT": zT_copied, "proj": gated,
                    "w": w_lo_ready, "gate": g_steps, "gateT": gate_stored, "xT": xT_lo_ready, "gk": gk_used}[kind]
            return name, u, n + 1

        def turn_bank(turn):
            return turn_ps[(TURNS.index(turn) - LOOP_TURN) % 2]

        def run(eng, item):
            for x in PRE + unit_items(0):
                item(0, *x)
            with eng.Fori(0, LOOPS) as hp:
                for u in BODY:
                    for x in unit_items(u):
                        item(hp, *x)
            for u in REST:
                for x in unit_items(u):
                    item(0, *x)
            for x in TAIL:
                item(0, *x)

        s_x = [ctx.enter_context(nc.semaphore(f"x_loaded{b}")) for b in range(B)]
        names = ("consts_loaded", "pj_loaded", "gw_loaded", "ident_zero", "ident_ready", "causal_ready", "ones_ready", "pow_ready", "var_eps_done",
                 "fixed_ready", "stats_done", "mv_done", "rstd_done", "xn_done",
                 "kmax_ready", "kmax_row_ready", "gw_step", "gw_ready", "max_seen", "probs_seen",)
        s = {n: ctx.enter_context(nc.semaphore(n)) for n in names}

        block = ctx.enter_context(nc.Block())

        @block.sync
        def _(sp):
            sp.dma_start(x_sb[:, 0:T, :], x_t[:, 0:T, :]).then_inc(s_x[0], 16)
            sp.dma_start(b_all[:, 0, :], b_cols[0], allow_slow_non_contiguous=True).then_inc(s["consts_loaded"], 16)
            sp.dma_start(b_all[:, 1, :], b_cols[1], allow_slow_non_contiguous=True).then_inc(s["consts_loaded"], 16)
            sp.dma_start(bv_all[:, :], bv_row.partition_broadcast(P)).then_inc(s["consts_loaded"], 16)
            for b in range(1, B):
                sp.dma_start(x_sb[:, b * T:(b + 1) * T, :], x_t[:, b * T:(b + 1) * T, :]).then_inc(s_x[b], 16)
            sp.dma_start(pj[:, :].rearrange("p (c e) -> p c e", e=E), proj.rearrange("(c p) e -> p c e", p=P)).then_inc(s["pj_loaded"], 16)

            def item(hp, kind, u, n):
                par = u % 2
                if (kind, n) == ("qk", 1):
                    wait(sp, hi_ready, hp, u, 4)
                    inc(sp.dma_start(QA[D:P, par, :, :].bitcast(F32), QA[0:D, par, :, :].bitcast(F32)), qA_filled)
                elif (kind, n) == ("qk", 3):
                    wait(sp, hi_ready, hp, u, 8)
                    inc(sp.dma_start(KB[0:D, par, :, :].bitcast(F32), KA[0:D, par, :, :].bitcast(F32)), kB_filled)
                elif kind == "maxT":
                    wait(sp, neg_max_ready, hp, u, n + 1)
                    inc(sp.dma_start(QB[D:D + 1, par, n, :].bitcast(F32), neg_max[:, n, :].bitcast(F32)), max_row[n])
                elif kind == "proj":
                    wait(sp, out_ready, hp, u, 1)
                    inc(sp.dma_start(out[u % B, bass.ds((hp + u // B) * P, P), :], out_sb[:, par, :]), out_written[par])

            for name in out_written:
                sp.sem_inc(count[name][0], 16)
            run(sp, item)
            for name in out_written:
                wait(sp, name, 0, UNITS, 0)

        @block.gpsimd
        def _(pool):
            def load_pair(pair):
                for i, w in enumerate(w_rows):
                    inc(pool.dma_start(w_nat[:, i, :], w[bass.ds(pair * P, P), :]), w_loaded)

            load_pair(0)
            pool.dma_start(kw, kern).then_inc(s["gw_loaded"], 16)
            pool.dma_start(la, lora_a).then_inc(s["gw_loaded"], 16)
            pool.dma_start(lb, lora_b).then_inc(s["gw_loaded"], 16)
            pool.dma_start(g_bias, bias.rearrange("(p a) -> p a", a=1)).then_inc(s["gw_loaded"], 16)
            pool.memset(minus_half, -0.5).then_inc(s["pow_ready"], 1)
            pool.memset(ident[:, :], 0.0).then_inc(s["ident_zero"], 1)
            pool.memset(causal[:, :], 0.0).then_inc(s["ident_zero"], 1)
            pool.wait_ge(s["ident_zero"], 2)
            pool.affine_select(out=ident[:, :], in_=ident[:, :], compare_op=ALU.not_equal, fill=1.0, base=0,
                               pattern=[[-1, P]], channel_multiplier=1).then_inc(s["ident_ready"], 1)
            pool.affine_select(out=causal[:, HALF - P:HALF], in_=causal[:, HALF - P:HALF], compare_op=ALU.is_ge,
                               fill=LOW, base=0, pattern=[[-1, P]], channel_multiplier=1).then_inc(s["causal_ready"], 1)
            pool.memset(ones_row, 1.0).then_inc(s["ones_ready"], 1)
            for par in range(2):
                pool.memset(V[:, par, :, :, D:D + 1], SCALE).then_inc(s["fixed_ready"], 1)
            pool.wait_ge(s["pow_ready"], 1)

            def item(hp, kind, u, n):
                if kind == "w" and n == 1:
                    wait(pool, turn_ready["w"], hp, u, 2)
                    load_pair((hp + u // B + 1) % HP)
                elif kind == "stats":
                    var = mv[:, n * T:(n + 1) * T, 1]
                    pool.wait_ge(s["var_eps_done"], n + 1)
                    pool.tensor_tensor(out=var, in0=var, in1=minus_half, op=ALU.pow).then_inc(s["rstd_done"], 1)
                elif kind == "score" and n % NPC in MASKED:
                    segments = PIECES[n % NPC]
                    slot = probs[:, n % SLOTS, :].rearrange("p (t n) -> p t n", n=P)
                    diag = slot[:, 0::3, :] if len(segments) == 2 else slot[:, 0:1, :]
                    wait(pool, probs_ready, hp, u, n + 1)
                    pool.sem_inc(s["probs_seen"], 1)
                    inc(pool.affine_select(out=diag, in_=diag, compare_op=ALU.is_ge, fill=0.0, base=0,
                                           pattern=[[0, len(segments)], [1, P]], channel_multiplier=-1), masked_ready)

            run(pool, item)
            wait(pool, w_loaded, 0, UNITS, 3)

        @block.scalar
        def _(act):
            act.wait_ge(s["consts_loaded"], 48)

            def item(hp, kind, u, n):
                turn, par = (kind, u, n), u % 2
                if kind == "score":
                    wait(act, scores_ready, hp, u, n + 1)
                    wait(act, probs_used, hp, u, n + 1 - SLOTS)
                    cols = P * sum(w for _, _, w in PIECES[n % NPC])
                    inc(nc.scalar.activation(probs[:, n % SLOTS, 0:cols], score_ps[n % 2][:, 0:cols], ACT.Exp,
                                             scale=1.0 / SCALE), probs_ready)
                elif kind == "qk":
                    which, half = n // 2, n % 2
                    wait(act, turn_ready[kind], hp, u, n + 1)
                    if u % B == 0 and n == 0:
                        wait(act, w_hi_ready, hp, u, 2)
                    for h in range(2):
                        dst = (QA, KA)[which][0:D, par, h, half * HALF:(half + 1) * HALF]
                        inc(nc.scalar.activation(dst, turn_bank(turn)[h * D:(h + 1) * D, :], ACT.Identity,
                                                 bias=b_act[:, which, h:h + 1]), hi_ready)
                elif kind == "zT":
                    wait(act, turn_ready[kind], hp, u, n + 1)
                    if n == 0:
                        wait(act, turn_ready["proj"], hp, u, 0)
                    for tp in range(2):
                        row = (2 * n + tp) * 16
                        src = turn_bank(turn)[:, tp * 2 * P:(tp + 1) * 2 * P].rearrange("p (h a c) -> p c h a", h=2, c=8)
                        ins = nc.scalar.copy(zT[:, :, :, row:row + 16], src)
                    inc(ins, zT_copied)
                elif kind == "w":
                    wait(act, turn_ready[kind], hp, u, n + 1)
                    cols = slice(0, 2 * P) if n == 0 else slice(2 * P, 3 * P)
                    if n == 0:
                        wait(act, hi_ready, hp, u, 0)
                        nc.scalar.copy(b_act[:, :, :], b_all[:, :, bass.ds((hp + u // B) * 2, 2)])
                    inc(nc.scalar.activation(wT_hi[:, cols], turn_bank(turn)[:, 0:cols.stop - cols.start], ACT.Copy),
                        w_hi_ready)
                elif kind == "xT":
                    wait(act, turn_ready[kind], hp, u, n + 1)
                    inc(nc.scalar.activation(xT_hi[:, n * HALF:(n + 1) * HALF], turn_bank(turn)[:, :], ACT.Copy),
                        xT_hi_ready)
                elif kind == "gate":
                    wait(act, turn_ready[kind], hp, u, 1)
                    if u == 0:
                        act.wait_ge(s["gw_loaded"], 64)
                    wait(act, gT_ready, hp, u, 0)
                    inc(nc.scalar.activation(g_exp[:, :], turn_bank(turn)[:, 0:P], ACT.Abs, bias=g_bias), g_abs_ready)
                    wait(act, g_abs_ready, hp, u, 1)
                    inc(nc.scalar.activation(g_exp[:, :], g_exp[:, :], ACT.Exp, scale=-1.0), g_exp_ready)
                elif kind == "gateT":
                    wait(act, turn_ready[kind], hp, u, 1)
                    wait(act, gated, hp, u, 0)
                    inc(nc.scalar.copy(gate_sb[:, :], turn_bank(turn)[:, 0:E]),
                        gate_stored)

            run(act, item)

        @block.vector
        def _(dve):
            dve.sem_inc(count[gated][0], 1)
            for par in range(2):
                nc.vector.memset(KB[D:D + 1, par, :, :].bitcast(F32), 1.0).then_inc(s["fixed_ready"], 1)
            dve.wait_ge(s["causal_ready"], 1)
            step = [0]

            def then(ins):
                step[0] += 1
                ins.then_inc(s["gw_step"], 1)
                dve.wait_ge(s["gw_step"], step[0])

            def gk_part(n, ps):
                if n == 0:
                    inc(nc.vector.reduce_max(kmax_row[0:1, 0:1], ps[0:1, 0:P], AX.X), gk_used)
                elif n == 1:
                    inc(nc.vector.tensor_copy(laT, ps[0:R, 0:P]), gk_used)
                elif n == 2:
                    inc(nc.vector.tensor_scalar(kmax[:, 1:2], ps[:, 0:1], 1.0 / QMAX, None, ALU.mult), gk_used)
                    wait(dve, gk_used, 0, 0, 3)
                    then(nc.vector.reciprocal(kmax[:, 2:3], kmax[:, 1:2]))
                    then(nc.vector.tensor_scalar(kw_q, kw, kmax[:, 2:3], None, ALU.mult))
                    then(nc.vector.tensor_scalar(kw_q, kw_q, ROUND, -ROUND, ALU.add, ALU.add))
                    then(nc.vector.tensor_scalar(kw_q, kw_q, QMIN, QMAX, ALU.max, ALU.min))
                else:
                    inc(nc.vector.scalar_tensor_tensor(out=kw_sum, in0=kw_q, scalar=kmax[:, 1:2], in1=ps[:, 0:P],
                                                       op0=ALU.mult, op1=ALU.add), gk_used)
                    wait(dve, gk_used, 0, 0, 4)
                    then(nc.vector.tensor_copy(gw_hi[:, :], kw_sum))
                    nc.vector.tensor_tensor(out=gw_lo[:, :], in0=kw_sum, in1=gw_hi[:, :].bitcast(F32), op=ALU.subtract
                                            ).then_inc(s["gw_ready"], 1)

            def row_max(hp, u, n):
                h, (i, _, keys, diagonal) = n // NMX, MAXES[n % NMX]
                col = i if diagonal else T + i - 4
                ps = max_ps[n % 2][:, 0:keys]
                if n % NMX == 0:
                    wait(dve, turn_ready["maxT"], hp, u, h + 1 - 2)
                wait(dve, maxes_ready, hp, u, n + 1)
                if diagonal:
                    dve.sem_inc(s["max_seen"], 1)
                    ins = nc.vector.tensor_tensor_reduce(out=ps, in0=ps, in1=causal[:, HALF - keys:HALF], scale=1.0,
                                                         scalar=LOW, op0=ALU.add, op1=ALU.max,
                                                         accum_out=mx[:, h, col:col + 1])
                else:
                    ins = nc.vector.reduce_max(mx[:, h, col:col + 1], ps, AX.X)
                inc(ins, maxes_used)
                if n % NMX == NMX - 1:
                    wait(dve, maxes_used, hp, u, n + 1)
                    inc(nc.vector.tensor_tensor(out=mx[:, h, 4:8], in0=mx[:, h, 4:8], in1=mx[:, h, 8:12], op=ALU.max),
                        mx_ready)

            def store_z(hp, u, h, half):
                ps = z_ps[half][:, 0:4 * (D + 1)].rearrange("p (t c) -> p t c", t=4)
                n = h * 2 + half + 1
                wait(dve, probs_used, hp, u, h * NPC + LAST_OF[half] + 1)
                inc(nc.vector.reciprocal(rden[:, half, :], ps[:, :, D]), rden_ready)
                if h == 0:
                    wait(dve, turn_ready["zT"], hp, u, half + 1 - 2)
                wait(dve, rden_ready, hp, u, n)
                for tp in range(2):
                    ins = nc.vector.tensor_tensor(
                        out=z[:, 2 * half + tp, h, :].rearrange("p (c d) -> p c d", c=2),
                        in0=ps[:, 2 * tp:2 * tp + 2, 0:D],
                        in1=rden[:, half, 2 * tp:2 * tp + 2].unsqueeze(2).to_broadcast([P, 2, D]), op=ALU.mult)
                inc(ins, z_stored)

            def item(hp, kind, u, n):
                turn, par = (kind, u, n), u % 2
                if kind == "stats":
                    dve.wait_ge(s_x[n], 16)
                    for t in range(n * T, (n + 1) * T):
                        nc.vector.bn_stats(stats[:, t, :], x_sb[:, t, :]).then_inc(s["stats_done"], 1)
                    for t in range(n * T, (n + 1) * T):
                        dve.wait_ge(s["stats_done"], t + 1)
                        nc.vector.bn_aggr(mv[:, t, :], stats[:, t, :]).then_inc(s["mv_done"], 1)
                    dve.wait_ge(s["mv_done"], (n + 1) * T)
                    nc.vector.tensor_scalar(mv[:, n * T:(n + 1) * T, 1], mv[:, n * T:(n + 1) * T, 1], EPS, None,
                                            ALU.add).then_inc(s["var_eps_done"], 1)
                    if n == B - 1:
                        dve.wait_ge(s["gw_loaded"], 64)
                        nc.vector.tensor_reduce(kmax[:, 0:1], kw, AX.X, ALU.max, apply_absolute_value=True
                                                ).then_inc(s["kmax_ready"], 1)
                elif kind == "norm":
                    dve.wait_ge(s["rstd_done"], n + 1)
                    for t in range(n * T, (n + 1) * T):
                        nc.vector.tensor_scalar(xn[:, t, :], x_sb[:, t, :], mv[:, t, 0:1], mv[:, t, 1:2],
                                                ALU.subtract, ALU.mult).then_inc(s["xn_done"], 1)
                elif kind == "xT":
                    cols = slice(n * HALF, (n + 1) * HALF)
                    wait(dve, xT_hi_ready, hp, u, n + 1)
                    inc(nc.vector.tensor_tensor(out=xT_lo[:, cols], in0=turn_bank(turn)[:, :],
                                                in1=xT_hi[:, cols].bitcast(F32), op=ALU.subtract), xT_lo_ready)
                elif kind == "gk":
                    wait(dve, turn_ready[kind], hp, u, n + 1)
                    gk_part(n, turn_bank(turn))
                elif kind == "pv" and n % NPC in (LAST_OF[0], LAST_OF[1]):
                    store_z(hp, u, n // NPC, int(n % NPC == LAST_OF[1]))
                elif kind == "max":
                    row_max(hp, u, n)
                elif kind == "qk":
                    which, half = n // 2, n % 2
                    cols = slice(half * HALF, (half + 1) * HALF)
                    wait(dve, hi_ready, hp, u, 2 * (n + 1))
                    if u % B == 0 and n == 0:
                        wait(dve, w_lo_ready, hp, u, 2)
                    for h in range(2):
                        hi = (QA, KA)[which][0:D, par, h, cols]
                        lo = (QB[0:D, par, h, cols], KA[D:P, par, h, cols])[which]
                        ins = nc.vector.scalar_tensor_tensor(out=lo, in0=turn_bank(turn)[h * D:(h + 1) * D, :],
                                                             scalar=b_dve[:, which, h:h + 1], in1=hi.bitcast(F32),
                                                             op0=ALU.add, op1=ALU.subtract)
                    inc(ins, lo_ready)
                elif kind == "v":
                    wait(dve, turn_ready[kind], hp, u, n + 1)
                    dst = V[:, par, 4 * n:4 * n + 4, :, 0:D]
                    inc(nc.vector.tensor_tensor(
                        out=dst, in0=turn_bank(turn)[:, :].rearrange("p (t h d) -> p t h d", t=4, h=2),
                        in1=bv_cur[:, :].rearrange("p (h d) -> p h d", h=2).unsqueeze(1).to_broadcast([P, 4, 2, D]),
                        op=ALU.add), v_stored)
                elif kind == "maxT":
                    wait(dve, turn_ready[kind], hp, u, n + 1)
                    wait(dve, max_row[n], hp, u, 0)
                    inc(nc.vector.tensor_scalar(neg_max[:, n, :], turn_bank(turn)[0:T, 0:P], -1.0, None, ALU.mult),
                        neg_max_ready)
                elif kind == "proj":
                    wait(dve, turn_ready[kind], hp, u, 1)
                    wait(dve, gate_stored, hp, u, 1)
                    wait(dve, out_written[par], hp, u, 0)
                    inc(nc.vector.tensor_tensor(out=out_sb[:, par, :], in0=turn_bank(turn)[:, 0:E],
                                                in1=gate_sb[:, :], op=ALU.mult), gated)
                    wait(dve, gated, hp, u, 1)
                    inc(nc.vector.tensor_tensor(out=out_sb[:, par, :], in0=out_sb[:, par, :],
                                                in1=x_sb[:, bass.ds(u % B * T + hp + u // B, 1), :], op=ALU.add),
                        out_ready)
                elif kind == "w":
                    cols = slice(0, 2 * P) if n == 0 else slice(2 * P, 3 * P)
                    pair = hp + u // B
                    if n == 0:
                        wait(dve, v_stored, hp, u - 1, 2)
                        nc.vector.tensor_copy(b_dve[:, :, :], b_all[:, :, bass.ds(pair * 2, 2)])
                        nc.vector.tensor_copy(bv_cur[:, :], bv_all[:, bass.ds(pair * P, P)])
                    wait(dve, w_hi_ready, hp, u, n + 1)
                    inc(nc.vector.tensor_tensor(out=wT_lo[:, cols], in0=turn_bank(turn)[:, 0:cols.stop - cols.start],
                                                in1=wT_hi[:, cols].bitcast(F32), op=ALU.subtract), w_lo_ready)
                elif kind == "gate":
                    wait(dve, g_abs_ready, hp, u, 1)
                    wait(dve, turn_ready["gateT"], hp, u, 0)
                    inc(nc.vector.tensor_scalar(gT[:, :], turn_bank(turn)[:, 0:P], g_bias, None, ALU.add), g_steps)
                elif kind == "silu":
                    if n == 0:
                        wait(dve, g_exp_ready, hp, u, 1)
                        inc(nc.vector.tensor_scalar(g_den[:, :], g_exp[:, :], 1.0, None, ALU.add), g_steps)
                        wait(dve, g_steps, hp, u, 2)
                        inc(nc.vector.scalar_tensor_tensor(out=g_exp[:, :], in0=gT[:, :], scalar=0.0, in1=g_exp[:, :],
                                                           op0=ALU.is_ge, op1=ALU.max), g_steps)
                    elif n == 1:
                        inc(nc.vector.reciprocal(g_den[:, :], g_den[:, :]), g_steps)
                    else:
                        wait(dve, g_steps, hp, u, 4)
                        inc(nc.vector.tensor_tensor(out=gT[:, :], in0=gT[:, :], in1=g_exp[:, :], op=ALU.mult), g_steps)
                        wait(dve, g_steps, hp, u, 5)
                        inc(nc.vector.tensor_tensor(out=gT[:, :], in0=gT[:, :], in1=g_den[:, :], op=ALU.mult),
                            gT_ready)

            dve.wait_ge(s["consts_loaded"], 48)
            run(dve, item)

        @block.tensor
        def _(pe):
            mm = nc.tensor.matmul
            pe.wait_ge(s["ident_ready"], 1)
            def three(out, w_hi, w_lo, m_hi, m_lo, **kw):
                mm(out, w_hi, m_hi, start=True, stop=False, **kw)
                mm(out, w_hi, m_lo, start=False, stop=False, **kw)
                return mm(out, w_lo, m_hi, start=False, stop=True, **kw)

            def item(hp, kind, u, n):
                turn, b, par = (kind, u, n), u % B, u % 2
                if kind == "score":
                    h, k = n // NPC, n % NPC
                    ps = score_ps[n % 2]
                    if k == 0:
                        wait(pe, max_row[h], hp, u, 1)
                        if h == 0:
                            wait(pe, kB_filled, hp, u, 1)
                        if u == 0 and h == 0:
                            pe.wait_ge(s["fixed_ready"], 4)
                    wait(pe, probs_ready, hp, u, n + 1 - 2)
                    at = 0
                    for j, s0, w in PIECES[k]:
                        keys, queries = slice(j * P, (j + 1) * P), slice(s0 * P, (s0 + w) * P)
                        dst = ps[:, at:at + w * P]
                        mm(dst, KA[:, par, h, keys], QA[:, par, h, queries], start=True, stop=False)
                        last = mm(dst, KB[:, par, h, keys], QB[:, par, h, queries], start=False, stop=True)
                        at += w * P
                    inc(last, scores_ready)
                elif kind == "pv":
                    h, k = n // NPC, n % NPC
                    half = int(k >= FIRST_OF[1])
                    first = k == FIRST_OF[half]
                    if n == 0:
                        wait(pe, v_stored, hp, u, 2)
                    if first:
                        wait(pe, z_stored, hp, u, h * 2 + half + 1 - 2)
                    if k in MASKED:
                        wait(pe, masked_ready, hp, u, h * len(MASKED) + MASKED.index(k) + 1)
                    else:
                        wait(pe, probs_ready, hp, u, n + 1)
                    at = 0
                    for j, s0, w in PIECES[k]:
                        i = s0
                        while i < s0 + w:
                            alone = i % 2
                            width = (1 if alone else 2) * P
                            for odd in range(2):
                                c = (i // 2 % 2 * 2 + odd) * (D + 1)
                                dst = z_ps[half][D if alone else 0:P, c:c + D + 1]
                                last = mm(dst, probs[:, n % SLOTS, at + odd:at + width:2], V[:, par, j, h, :],
                                          start=first, stop=j == i or j == i + 1, skip_group_check=True)
                                first = False
                            at += width
                            i += 1 if alone else 2
                    inc(last, probs_used)
                elif kind == "max":
                    h, (i, key0, keys, _) = n // NMX, MAXES[n % NMX]
                    if n in (0, 4):
                        wait(pe, lo_ready, hp, u, 4 if n else 3)
                    if n == 0:
                        wait(pe, qA_filled, hp, u, 1)
                    wait(pe, maxes_used, hp, u, n + 1 - 2)
                    inc(mm(max_ps[n % 2][:, 0:keys], QA[:, par, h, i * P:(i + 1) * P],
                           KA[:, par, h, key0:key0 + keys], start=True, stop=True), maxes_ready)
                elif kind in TURN_KINDS:
                    if TURNS.index(turn) >= 2:
                        name, before, at = freed(TURNS[TURNS.index(turn) - 2])
                        wait(pe, name, hp, before, at)
                    ps = turn_bank(turn)
                    if kind == "qk":
                        which, half = n // 2, n % 2
                        if b == 0 and n == 0:
                            wait(pe, w_lo_ready, hp, u, 2)
                        if u == 0:
                            wait(pe, xT_lo_ready, 0, 0, n % 2 + 1)
                        if u == 1 and n == 0:
                            pe.wait_ge(count[xT_lo_ready][0], 2 * 2)
                        col0 = b * S + half * HALF
                        w = slice(which * P, (which + 1) * P)
                        last = three(ps[:, :], wT_hi[:, w], wT_lo[:, w], xT_hi[:, col0:col0 + HALF],
                                     xT_lo[:, col0:col0 + HALF])
                    elif kind == "v":
                        for i in range(4):
                            tok = b * S + (4 * n + i) * P
                            last = three(ps[:, i * P:(i + 1) * P], xT_hi[:, tok:tok + P], xT_lo[:, tok:tok + P],
                                         wT_hi[:, 2 * P:3 * P], wT_lo[:, 2 * P:3 * P])
                    elif kind == "maxT":
                        wait(pe, mx_ready, hp, u, n + 1)
                        last = nc.tensor.transpose(ps[0:T, 0:P], mx[:, n, 0:T], ident[:, :])
                    elif kind == "zT":
                        wait(pe, z_stored, hp, u, 2 + n + 1)
                        for tp in range(2):
                            for h in range(2):
                                c = (tp * 2 + h) * P
                                last = nc.tensor.transpose(ps[:, c:c + P], z[:, 2 * n + tp, h, :], ident[:, :])
                    elif kind == "proj":
                        wait(pe, zT_copied, hp, u, 2)
                        if u == 0:
                            pe.wait_ge(s["pj_loaded"], 16)
                        for c in range(8):
                            last = mm(ps[:, 0:E], zT[:, c, :, :].rearrange("p h a -> p (h a)"),
                                      pj[:, c * E:(c + 1) * E], start=c == 0, stop=c == 7)
                    elif kind == "w":
                        if n == 0:
                            wait(pe, w_loaded, hp, u, 3)
                        for i in (0, 1) if n == 0 else (2,):
                            c = (i % 2) * P
                            last = nc.tensor.transpose(ps[:, c:c + P], w_nat[:, i, :], ident[:, :])
                    elif kind == "gate":
                        if u == 0:
                            pe.wait_ge(s["gw_ready"], 1)
                        rows = bass.ds((hp + u // B) * P + b * S, P)
                        last = three(ps[:, 0:P], gw_hi[:, :], gw_lo[:, :], xT_hi[:, rows], xT_lo[:, rows])
                    elif kind == "gateT":
                        wait(pe, gT_ready, hp, u, 1)
                        last = nc.tensor.transpose(ps[:, 0:P], gT[:, :], ident[:, :])
                    elif kind == "xT":
                        pe.wait_ge(s["xn_done"], (n + 1) * 4)
                        for i in range(4):
                            last = nc.tensor.transpose(ps[:, i * P:(i + 1) * P], xn[:, n * 4 + i, :], ident[:, :])
                    elif kind == "gk":
                        if n == 0:
                            pe.wait_ge(s["kmax_ready"], 1)
                            last = nc.tensor.transpose(ps[0:1, 0:P], kmax[:, 0:1], ident[:, :])
                        elif n == 1:
                            last = nc.tensor.transpose(ps[0:R, 0:P], la, ident[:, :])
                        elif n == 2:
                            wait(pe, gk_used, 0, 0, 1)
                            pe.wait_ge(s["ones_ready"], 1)
                            last = mm(ps[:, 0:1], ones_row, kmax_row[0:1, 0:1], start=True, stop=True)
                        else:
                            wait(pe, gk_used, 0, 0, 2)
                            last = mm(ps[:, 0:P], laT, lb, start=True, stop=True)
                    inc(last, turn_ready[kind])

            run(pe, item)


_INS = ["L0_attn_x", "L0_attn_Wq", "L0_attn_bq", "L0_attn_Wk", "L0_attn_bk", "L0_attn_Wv", "L0_attn_bv",
        "L0_attn_proj", "L0_ffn_kernel", "L0_ffn_bias", "L0_ffn_a", "L0_ffn_b"]


def kernel(**inputs):
    import numpy as _np
    import concourse.bacc as _bacc
    from concourse import mybir as _mybir
    from concourse.bass_utils import run_bass_kernel_spmd as _run

    nc = _bacc.Bacc("TRN2", target_bir_lowering=False, num_devices=1)
    arrays, args = {}, []
    for name in _INS:
        a = _np.ascontiguousarray(inputs[name])
        arrays[f"in_{name}_dram"] = a
        args.append(nc.dram_tensor(f"in_{name}_dram", a.shape, _mybir.dt.from_np(a.dtype), kind="ExternalInput").ap())
    args.append(nc.dram_tensor("out_dram", (B, S, E), _mybir.dt.float32, kind="ExternalOutput").ap())
    attention_kernel(nc, *args)
    r = _run(nc, [arrays], core_ids=[0])
    return r.results[0]["out_dram"]
```

```python
import math

import concourse.bass as bass
from concourse import mybir
from contextlib import ExitStack

F32 = mybir.dt.float32
F32R = mybir.dt.float32r
F16 = mybir.dt.float16
ALU = mybir.AluOpType
ACT = mybir.ActivationFunctionType
AX = mybir.AxisListType

P = 128
B, S, E = 4, 1024, 128
H, D = 16, 64
HP = H // 2
T = S // P
HALF = 4 * P
R = 16
EPS = 1e-5
SCALE = float(D) ** 0.5
QMAX, QMIN = 7.0, -8.0
ROUND = 1.5 * 2.0 ** 23
LOW = -3.0e38

PIECES = [[(0, 0, 4)], [(1, 1, 3), (3, 3, 1)], [(2, 2, 2)],
          [(0, 4, 4)], [(1, 4, 4)], [(2, 4, 4)], [(3, 4, 4)], [(4, 4, 4)], [(5, 5, 3), (7, 7, 1)], [(6, 6, 2)]]
NPC = len(PIECES)
FIRST_OF, LAST_OF = {0: 0, 1: 3}, {0: 2, 1: 9}
MASKED = [k for k in range(NPC) if any(j == s for j, s, _ in PIECES[k])]
MAXES = [(i, 0, P * (i + 1), True) for i in range(4)]
for _i in range(4, T):
    MAXES += [(_i, 0, HALF, False), (_i, HALF, P * (_i - 3), True)]
NMX = len(MAXES)
SPLIT_LAG = 1
LAG = 4
SLOTS = 4
PART_SLOTS = 5
V_TOP = 2.0 ** 14
TINY = 1.0e-34
GAIN = 32.0


UNITS = B * HP
BODY = range(1, 1 + B)
LOOPS = (UNITS - 1) // B
REST = range(1 + B * LOOPS, UNITS)

SLOTS_A_UNIT = 2 * NPC
TIMES = [
    ("maxT", (16, 24), 1),
    ("neg_max", (16, 24), 1),
    ("gate", (12,), 0),
    ("g_exp", (12,), 0),
    ("g_y", (12,), 0),
    ("silu", (19, 20, 21), 0),
    ("gateT", (23,), 0),
    ("gate_copy", (24,), 0),
    ("z", (7, 15, 16, 24), 0),
    ("zT", (18, 26), 0),
    ("zT_copy", (18, 26), 0),
    ("proj", (28,), 0),
    ("out", (29,), 0),
    ("qk", (0, 2, 5, 6), 1),
    ("qk_lo", (1, 3, 6, 7), 1),
    ("v", (7, 11), 1),
    ("v_add", (7, 11), 1),
    ("v1", (8, 12), 1),
    ("v2", (10, 13), 1),
]
MAX_AT = (8, 9, 9, 9, 11, 11, 11, 12, 12, 14, 14, 14,
          15, 15, 16, 17, 17, 18, 19, 19, 19, 19, 21, 22)
W_AT = (11, 12)
SPARE = 2


def unit_items(u):
    items = []

    def due(slots, ahead):
        found = [(u + ahead - slot // SLOTS_A_UNIT, n) for n, slot in enumerate(slots) if slot % SLOTS_A_UNIT == k]
        return [x for x in found if 0 <= x[0] < UNITS]

    for k in range(SLOTS_A_UNIT):
        maxes = [x for x in due(MAX_AT, 1) if x[0]]
        items.append(("score", u, k))
        items += [("max", *x) for x in maxes[:1]]
        items += [("split", *x) for x in due([n + SPLIT_LAG for n in range(SLOTS_A_UNIT)], 0)]
        items += [("pv", *x) for x in due([n + LAG for n in range(SLOTS_A_UNIT)], 0)]
        for kind, slots, ahead in TIMES:
            items += [(kind, *x) for x in due(slots, ahead)]
        if u == 0:
            items += FIRST_UNIT.get(k, [])
        items += [("max", *x) for x in maxes[1:]]
        if u % B == 2 and u + 2 < UNITS and k in W_AT:
            items.append(("w", u + 2, W_AT.index(k)))
        if u % B == 3 and k == 10:
            items += [("spare", u, n) for n in range(SPARE)]
    return items


PRE = [("stats", 0, 0), ("w", 0, 0), ("w", 0, 1), ("norm", 0, 0), ("v_bound", 0, 0), ("stats", 0, 1)]
PRE += [("xT", 0, 0), ("xT", 0, 1), ("qk", 0, 0), ("qk_lo", 0, 0), ("norm", 0, 1), ("qk", 0, 1), ("qk_lo", 0, 1)]
PRE += [("xT", 0, 2), ("qk", 0, 2), ("qk_lo", 0, 2), ("v_bound", 0, 1), ("xT", 0, 3), ("qk", 0, 3), ("qk_lo", 0, 3)]
PRE += [(kind, 0, n) for kind in ("v", "v_add", "v1") for n in range(2)]
PRE += [("max", 0, n) for n in range(NMX)] + [("maxT", 0, 0), ("neg_max", 0, 0)]
PRE += [("v2", 0, n) for n in range(2)]
PRE += [("max", 0, n) for n in range(NMX, 2 * NMX)]
FIRST_UNIT = {
    2: [("stats", 0, 2)],
    4: [("norm", 0, 2)],
    7: [("xT", 0, 4), ("xT", 0, 5)],
    8: [("stats", 0, 3), ("gk", 0, 0), ("gk", 0, 1)],
    9: [("norm", 0, 3)],
    10: [("gk", 0, 2)],
    11: [("xT", 0, 6), ("gk", 0, 3), ("xT", 0, 7)],
}
TAIL = [("split", UNITS - 1, 2 * NPC - n) for n in range(SPLIT_LAG, 0, -1)]
TAIL += [("pv", UNITS - 1, 2 * NPC - n) for n in range(LAG, 0, -1)]
TAIL += [(kind, UNITS - 1, n) for kind, n in (("z", 3), ("silu", 1), ("silu", 2), ("gateT", 0), ("gate_copy", 0),
                                              ("zT", 1), ("zT_copy", 1), ("proj", 0), ("out", 0))]

RING = 4
TURN_KINDS = ("qk", "v", "max", "maxT", "zT", "proj", "w", "gate", "gateT", "xT", "gk", "v_bound", "spare")
TURNS = [x for x in PRE + [y for u in range(UNITS) for y in unit_items(u)] + TAIL if x[0] in TURN_KINDS]
PERIOD = sum(x[0] in TURN_KINDS for u in BODY for x in unit_items(u))
assert PERIOD % RING == 0
TURN_OF = {x: n for n, x in enumerate(TURNS)}
LAST_TURN = {}
for _n, _x in enumerate(TURNS):
    _back = [y for y in TURNS[_n % RING:_n:RING] if y[0] != "spare"]
    LAST_TURN[_x] = _back[-1] if _back else None
PER_PAIR = ("w",)


def attention_kernel(nc, x, Wq, bq, Wk, bk, Wv, bv, proj, kern, bias, lora_a, lora_b, out):
    x_t = x.rearrange("b (t p) e -> p (b t) e", p=P)
    w_rows = [w.rearrange("h d e -> (h d) e") for w in (Wq, Wk, Wv)]
    b_cols = [w.rearrange("h d -> d h") for w in (bq, bk)]
    bv_row = bv.rearrange("h d -> (h d)").rearrange("(a n) -> a n", a=1)

    ctx = ExitStack()
    with ctx:
        def sb(name, shape, dt=F32):
            return ctx.enter_context(nc.sbuf_tensor(name, shape, dt))

        x_sb = sb("x_sb", [P, B * T, E])
        xn = sb("xn", [P, B * T, E])
        gate_sb = sb("gate_sb", [P, E])
        out_sb = sb("out_sb", [P, 2, E])
        xT_hi = sb("xT_hi", [P, B * S], F32R)
        xT_lo = sb("xT_lo", [P, B * S], F32R)
        w_nat = sb("w_nat", [P, 3, E])
        wT_hi = sb("wT_hi", [P, 3 * P], F32R)
        wT_lo = sb("wT_lo", [P, 3 * P], F32R)
        b_all = sb("b_all", [D, 2, H])
        b_act = sb("b_act", [D, 2, 2])
        b_dve = sb("b_dve", [D, 2, 2])
        bv_all = sb("bv_all", [P, H * D])
        bv_cur = sb("bv_cur", [P, P])
        pj = sb("pj", [P, HP * E])
        QA = sb("QA", [P, 2, 2, S], F32R)
        KA = sb("KA", [P, 2, 2, S], F32R)
        QB = sb("QB", [D + 1, 2, 2, S], F32R)
        KB = sb("KB", [D + 1, 2, 2, S], F32R)
        V1 = sb("V1", [P, 2, T, 2, D + 1], F16)
        V2 = sb("V2", [P, 2, T, 2, D], F16)
        v_sb = sb("v_sb", [P, 2, HALF])
        wv_all = sb("wv_all", [P, HP, E])
        v_max = sb("v_max", [P, 4])
        v_scale, v_unscale = sb("v_scale", [P, 1]), sb("v_unscale", [P, 1])
        probs = sb("probs", [P, SLOTS, HALF])
        p_hi = sb("p_hi", [P, PART_SLOTS, HALF], F16)
        p_lo = sb("p_lo", [P, PART_SLOTS, HALF], F16)
        z = sb("z", [P, 2, 4, P])
        zT = sb("zT", [P, 8, 2, D])
        mx = sb("mx", [P, 2, 12])
        neg_max = sb("neg_max", [T, 2, P], F32R)
        rden = sb("rden", [P, 2, 4])
        causal = sb("causal", [P, HALF])
        ident = sb("ident", [P, P])
        gw_hi = sb("gw_hi", [P, P], F32R)
        gw_lo = sb("gw_lo", [P, P], F32R)
        g_bias = sb("g_bias", [P, 1])[:, :]
        g_exp = sb("g_exp", [P, P])
        g_den = sb("g_den", [P, P])
        gT = sb("gT", [P, P])
        stats = sb("stats", [P, B * T, 6])
        mv = sb("mv", [P, B * T, 2])
        kw = sb("kw", [P, P])[:, :]
        kw_q = sb("kw_q", [P, P])[:, :]
        kw_sum = sb("kw_sum", [P, P])[:, :]
        la = sb("la", [P, R])[:, :]
        laT = sb("laT", [R, P])[:, :]
        lb = sb("lb", [R, P])[:, :]
        kmax = sb("kmax", [P, 8])[:, :]
        minus_half = sb("minus_half", [P, T])[:, :]
        ones_row = sb("ones_row", [1, P])[:, :]
        kmax_row = sb("kmax_row", [1, 8])[:, :]

        bank = [ctx.enter_context(nc.psum_tensor(f"bank{i}", [P, HALF], F32)) for i in range(8)]
        score_ps, z_ps, turn_ps = bank[0:2], bank[2:4], bank[4:8]

        count = {}

        def sem(name, per, span=1, weight=1, lead=0):
            count[name] = (ctx.enter_context(nc.semaphore(name)), per, span, weight, lead)
            return name

        scores_ready = sem("scores_ready", 2 * NPC)
        probs_used = sem("probs_used", 2 * NPC)
        maxes_ready = sem("maxes_ready", 2 * NMX)
        turns = dict(qk=4, v=2, maxT=2, zT=2, proj=1, w=2, gate=1, gateT=1, xT=2 * B, gk=4, v_bound=2)
        turn_ready = {k: sem(f"{k}_ready", n, span=B if k in PER_PAIR else 1) for k, n in turns.items()}
        probs_ready = sem("probs_ready", 2 * NPC)
        p_hi_ready = sem("p_hi_ready", 2 * NPC)
        v1_ready = sem("v1_ready", 2)
        hi_ready = sem("hi_ready", 4 * 2)
        zT_copied = sem("zT_copied", 2)
        w_hi_ready = sem("w_hi_ready", 2, span=B)
        xT_hi_ready = sem("xT_hi_ready", 2 * B)
        g_abs_ready = sem("g_abs_ready", 1)
        g_exp_ready = sem("g_exp_ready", 1)
        gate_stored = sem("gate_stored", 1)
        lo_ready = sem("lo_ready", 4)
        v_stored = sem("v_stored", 2)
        v2_ready = sem("v2_ready", 2)
        v_bound_used = sem("v_bound_used", 2)
        maxes_used = sem("maxes_used", 2 * NMX)
        mx_ready = sem("mx_ready", 2)
        neg_max_ready = sem("neg_max_ready", 2)
        rden_ready = sem("rden_ready", 4)
        z_stored = sem("z_stored", 4)
        gated = sem("gated", 1, lead=1)
        out_ready = sem("out_ready", 1)
        w_lo_ready = sem("w_lo_ready", 2, span=B)
        xT_lo_ready = sem("xT_lo_ready", 2 * B)
        gk_used = sem("gk_used", 4)
        g_steps = sem("g_steps", 5)
        gT_ready = sem("gT_ready", 1)
        masked_ready = sem("masked_ready", 2 * len(MASKED))
        p_lo_ready = sem("p_lo_ready", 2 * NPC)
        qA_filled = sem("qA_filled", 1, weight=16)
        kB_filled = sem("kB_filled", 1, weight=16)
        max_row = [sem(f"max_row{h}", 1, weight=16) for h in range(2)]
        w_loaded = sem("w_loaded", 3, span=B, weight=16)
        out_written = [sem(f"out_written{par}", 1, span=2, weight=16, lead=1) for par in range(2)]

        def by_head(ap):
            return ap.rearrange("p (t h d) -> p t h d", t=4, h=2)

        def inc(ins, name):
            ins.then_inc(count[name][0], count[name][3])

        def wait(eng, name, hp, u, n):
            s, per, span, weight, lead = count[name]
            fixed = (u // span * per + n + lead) * weight
            if isinstance(hp, int):
                assert hp == 0
                if fixed > 0:
                    eng.wait_ge(s, fixed)
            else:
                assert fixed > 0, (name, u, n)
                eng.wait_ge(s, hp * (B // span * per * weight) + fixed)

        def freed(turn):
            kind, u, n = turn
            name = {"qk": lo_ready, "v": v_stored, "maxT": neg_max_ready, "zT": zT_copied, "proj": gated,
                    "max": maxes_used, "w": w_lo_ready, "gate": g_steps, "gateT": gate_stored, "xT": xT_lo_ready, "gk": gk_used,
                    "v_bound": v_bound_used}[kind]
            return name, u, n + 1

        def turn_bank(turn):
            return turn_ps[TURN_OF[turn] % RING]

        def run(eng, item):
            for x in PRE + unit_items(0):
                item(0, *x)
            with eng.Fori(0, LOOPS) as hp:
                for u in BODY:
                    for x in unit_items(u):
                        item(hp, *x)
            for u in REST:
                for x in unit_items(u):
                    item(0, *x)
            for x in TAIL:
                item(0, *x)

        s_x = [ctx.enter_context(nc.semaphore(f"x_loaded{b}")) for b in range(B)]
        names = ("consts_loaded", "pj_loaded", "gw_loaded", "ident_zero", "ident_ready", "causal_ready", "ones_ready", "pow_ready", "var_eps_done",
                 "fixed_ready", "stats_done", "mv_done", "rstd_done", "xn_done",
                 "kmax_ready", "kmax_row_ready", "wv_loaded", "v_max_ready", "gw_step", "gw_ready", "max_seen", "probs_seen",)
        s = {n: ctx.enter_context(nc.semaphore(n)) for n in names}

        block = ctx.enter_context(nc.Block())

        @block.sync
        def _(sp):
            sp.dma_start(x_sb[:, 0:T, :], x_t[:, 0:T, :]).then_inc(s_x[0], 16)

            def load_pair(pair):
                for i, w in enumerate(w_rows):
                    inc(sp.dma_start(w_nat[:, i, :], w[bass.ds(pair * P, P), :]), w_loaded)

            load_pair(0)
            sp.dma_start(b_all[:, 0, :], b_cols[0], allow_slow_non_contiguous=True).then_inc(s["consts_loaded"], 16)
            sp.dma_start(b_all[:, 1, :], b_cols[1], allow_slow_non_contiguous=True).then_inc(s["consts_loaded"], 16)
            sp.dma_start(bv_all[:, :], bv_row.partition_broadcast(P)).then_inc(s["consts_loaded"], 16)
            sp.dma_start(wv_all[:, :, :], w_rows[2].rearrange("(c p) e -> p c e", p=P)).then_inc(s["wv_loaded"], 16)
            for b in range(1, B):
                sp.dma_start(x_sb[:, b * T:(b + 1) * T, :], x_t[:, b * T:(b + 1) * T, :]).then_inc(s_x[b], 16)
            for to, what in ((kw, kern), (la, lora_a), (lb, lora_b), (g_bias, bias.rearrange("(p a) -> p a", a=1))):
                sp.dma_start(to, what).then_inc(s["gw_loaded"], 16)
            sp.dma_start(pj[:, :].rearrange("p (c e) -> p c e", e=E), proj.rearrange("(c p) e -> p c e", p=P)).then_inc(s["pj_loaded"], 16)

            def item(hp, kind, u, n):
                par = u % 2
                if (kind, n) == ("qk", 1):
                    wait(sp, hi_ready, hp, u, 4)
                    inc(sp.dma_start(QA[D:P, par, :, :].bitcast(F32), QA[0:D, par, :, :].bitcast(F32)), qA_filled)
                elif (kind, n) == ("qk", 3):
                    wait(sp, hi_ready, hp, u, 8)
                    inc(sp.dma_start(KB[0:D, par, :, :].bitcast(F32), KA[0:D, par, :, :].bitcast(F32)), kB_filled)
                elif kind == "neg_max":
                    wait(sp, neg_max_ready, hp, u, n + 1)
                    inc(sp.dma_start(QB[D:D + 1, par, n, :].bitcast(F32), neg_max[:, n, :].bitcast(F32)), max_row[n])
                elif kind == "w" and n == 1:
                    wait(sp, turn_ready["w"], hp, u, 2)
                    load_pair((hp + u // B + 1) % HP)
                elif kind == "out":
                    wait(sp, out_ready, hp, u, 1)
                    inc(sp.dma_start(out[u % B, bass.ds((hp + u // B) * P, P), :], out_sb[:, par, :]), out_written[par])

            for name in out_written:
                sp.sem_inc(count[name][0], 16)
            run(sp, item)
            for name in out_written:
                wait(sp, name, 0, UNITS, 0)
            wait(sp, w_loaded, 0, UNITS, 3)

        @block.gpsimd
        def _(pool):
            pool.memset(minus_half, -0.5).then_inc(s["pow_ready"], 1)
            pool.memset(ident[:, :], 0.0).then_inc(s["ident_zero"], 1)
            pool.memset(causal[:, :], 0.0).then_inc(s["ident_zero"], 1)
            pool.wait_ge(s["ident_zero"], 2)
            pool.affine_select(out=ident[:, :], in_=ident[:, :], compare_op=ALU.not_equal, fill=1.0, base=0,
                               pattern=[[-1, P]], channel_multiplier=1).then_inc(s["ident_ready"], 1)
            pool.affine_select(out=causal[:, HALF - P:HALF], in_=causal[:, HALF - P:HALF], compare_op=ALU.is_ge,
                               fill=LOW, base=0, pattern=[[-1, P]], channel_multiplier=1).then_inc(s["causal_ready"], 1)
            pool.memset(ones_row, 1.0).then_inc(s["ones_ready"], 1)
            for par in range(2):
                pool.memset(V1[:, par, :, :, D:D + 1], SCALE).then_inc(s["fixed_ready"], 1)
            pool.wait_ge(s["pow_ready"], 1)

            def item(hp, kind, u, n):
                if kind == "split":
                    cols = P * sum(w for _, _, w in PIECES[n % NPC])
                    wait(pool, p_hi_ready, hp, u, n + 1)
                    inc(pool.tensor_tensor(out=p_lo[:, n % PART_SLOTS, 0:cols], in0=probs[:, n % SLOTS, 0:cols],
                                           in1=p_hi[:, n % PART_SLOTS, 0:cols], op=ALU.subtract), p_lo_ready)
                elif kind == "stats":
                    var = mv[:, n * T:(n + 1) * T, 1]
                    pool.wait_ge(s["var_eps_done"], n + 1)
                    pool.tensor_tensor(out=var, in0=var, in1=minus_half, op=ALU.pow).then_inc(s["rstd_done"], 1)
                elif kind == "score" and n % NPC in MASKED:
                    segments = PIECES[n % NPC]
                    slot = probs[:, n % SLOTS, :].rearrange("p (t n) -> p t n", n=P)
                    diag = slot[:, 0::3, :] if len(segments) == 2 else slot[:, 0:1, :]
                    wait(pool, probs_ready, hp, u, n + 1)
                    pool.sem_inc(s["probs_seen"], 1)
                    inc(pool.affine_select(out=diag, in_=diag, compare_op=ALU.is_ge, fill=0.0, base=0,
                                           pattern=[[0, len(segments)], [1, P]], channel_multiplier=-1), masked_ready)

            run(pool, item)

        @block.scalar
        def _(act):
            act.wait_ge(s["consts_loaded"], 48)

            def item(hp, kind, u, n):
                turn, par = (kind, u, n), u % 2
                if kind == "score":
                    wait(act, scores_ready, hp, u, n + 1)
                    wait(act, p_lo_ready, hp, u, n + 1 - SLOTS)
                    cols = P * sum(w for _, _, w in PIECES[n % NPC])
                    inc(nc.scalar.activation(probs[:, n % SLOTS, 0:cols], score_ps[n % 2][:, 0:cols], ACT.Exp,
                                             scale=1.0 / SCALE), probs_ready)
                elif kind == "split":
                    if n % NPC in MASKED:
                        wait(act, masked_ready, hp, u, n // NPC * len(MASKED) + MASKED.index(n % NPC) + 1)
                    else:
                        wait(act, probs_ready, hp, u, n + 1)
                    wait(act, probs_used, hp, u, n + 1 - PART_SLOTS)
                    cols = P * sum(w for _, _, w in PIECES[n % NPC])
                    inc(nc.scalar.activation(p_hi[:, n % PART_SLOTS, 0:cols], probs[:, n % SLOTS, 0:cols], ACT.Copy),
                        p_hi_ready)
                elif kind == "v1":
                    wait(act, v_stored, hp, u, n + 1)
                    inc(nc.scalar.activation(V1[:, par, 4 * n:4 * n + 4, :, 0:D], by_head(v_sb[:, n, :]), ACT.Copy),
                        v1_ready)
                elif kind == "qk":
                    which, half = n // 2, n % 2
                    wait(act, turn_ready[kind], hp, u, n + 1)
                    if u % B == 0 and n == 0:
                        wait(act, w_hi_ready, hp, u, 2)
                    for h in range(2):
                        dst = (QA, KA)[which][0:D, par, h, half * HALF:(half + 1) * HALF]
                        inc(nc.scalar.activation(dst, turn_bank(turn)[h * D:(h + 1) * D, :], ACT.Identity,
                                                 bias=b_act[:, which, h:h + 1]), hi_ready)
                elif kind == "zT_copy":
                    wait(act, turn_ready["zT"], hp, u, n + 1)
                    if n == 0:
                        wait(act, turn_ready["proj"], hp, u, 0)
                    for tp in range(2):
                        row = (2 * n + tp) * 16
                        src = turn_bank(("zT", u, n))[:, tp * 2 * P:(tp + 1) * 2 * P].rearrange("p (h a c) -> p c h a", h=2, c=8)
                        ins = nc.scalar.copy(zT[:, :, :, row:row + 16], src)
                    inc(ins, zT_copied)
                elif kind == "w":
                    wait(act, turn_ready[kind], hp, u, n + 1)
                    cols = slice(0, 2 * P) if n == 0 else slice(2 * P, 3 * P)
                    if n == 0:
                        wait(act, hi_ready, hp, u, 0)
                        nc.scalar.copy(b_act[:, :, :], b_all[:, :, bass.ds((hp + u // B) * 2, 2)])
                    inc(nc.scalar.activation(wT_hi[:, cols], turn_bank(turn)[:, 0:cols.stop - cols.start], ACT.Copy),
                        w_hi_ready)
                elif kind == "xT":
                    wait(act, turn_ready[kind], hp, u, n + 1)
                    inc(nc.scalar.activation(xT_hi[:, n * HALF:(n + 1) * HALF], turn_bank(turn)[:, :], ACT.Copy),
                        xT_hi_ready)
                elif kind == "g_exp":
                    wait(act, turn_ready["gate"], hp, u, 1)
                    if u == 0:
                        act.wait_ge(s["gw_loaded"], 64)
                    wait(act, gT_ready, hp, u, 0)
                    inc(nc.scalar.activation(g_exp[:, :], turn_bank(("gate", u, 0))[:, 0:P], ACT.Abs, bias=g_bias), g_abs_ready)
                    wait(act, g_abs_ready, hp, u, 1)
                    inc(nc.scalar.activation(g_exp[:, :], g_exp[:, :], ACT.Exp, scale=-1.0), g_exp_ready)
                elif kind == "gate_copy":
                    wait(act, turn_ready["gateT"], hp, u, 1)
                    wait(act, gated, hp, u, 0)
                    inc(nc.scalar.copy(gate_sb[:, :], turn_bank(("gateT", u, 0))[:, 0:E]),
                        gate_stored)

            run(act, item)

        @block.vector
        def _(dve):
            dve.sem_inc(count[gated][0], 1)
            for par in range(2):
                nc.vector.memset(KB[D:D + 1, par, :, :].bitcast(F32), 1.0).then_inc(s["fixed_ready"], 1)
            step = [0]

            def then(ins):
                step[0] += 1
                ins.then_inc(s["gw_step"], 1)
                dve.wait_ge(s["gw_step"], step[0])

            def gk_part(n, ps):
                if n == 0:
                    inc(nc.vector.reduce_max(kmax_row[0:1, 0:1], ps[0:1, 0:P], AX.X), gk_used)
                elif n == 1:
                    inc(nc.vector.tensor_copy(laT, ps[0:R, 0:P]), gk_used)
                elif n == 2:
                    inc(nc.vector.tensor_scalar(kmax[:, 1:2], ps[:, 0:1], 1.0 / QMAX, None, ALU.mult), gk_used)
                    wait(dve, gk_used, 0, 0, 3)
                    then(nc.vector.reciprocal(kmax[:, 2:3], kmax[:, 1:2]))
                    then(nc.vector.tensor_scalar(kw_q, kw, kmax[:, 2:3], None, ALU.mult))
                    then(nc.vector.tensor_scalar(kw_q, kw_q, ROUND, -ROUND, ALU.add, ALU.add))
                    then(nc.vector.tensor_scalar(kw_q, kw_q, QMIN, QMAX, ALU.max, ALU.min))
                else:
                    inc(nc.vector.scalar_tensor_tensor(out=kw_sum, in0=kw_q, scalar=kmax[:, 1:2], in1=ps[:, 0:P],
                                                       op0=ALU.mult, op1=ALU.add), gk_used)
                    wait(dve, gk_used, 0, 0, 4)
                    then(nc.vector.tensor_copy(gw_hi[:, :], kw_sum))
                    nc.vector.tensor_tensor(out=gw_lo[:, :], in0=kw_sum, in1=gw_hi[:, :].bitcast(F32), op=ALU.subtract
                                            ).then_inc(s["gw_ready"], 1)

            def row_max(hp, u, n):
                h, (i, _, keys, diagonal) = n // NMX, MAXES[n % NMX]
                col = i if diagonal else T + i - 4
                if u == 0 and n == 0:
                    dve.wait_ge(s["causal_ready"], 1)
                ps = turn_bank(("max", u, n))[:, 0:keys]
                if n % NMX == 0:
                    wait(dve, turn_ready["maxT"], hp, u, h + 1 - 2)
                wait(dve, maxes_ready, hp, u, n + 1)
                if diagonal:
                    dve.sem_inc(s["max_seen"], 1)
                    ins = nc.vector.tensor_tensor_reduce(out=ps, in0=ps, in1=causal[:, HALF - keys:HALF], scale=1.0,
                                                         scalar=LOW, op0=ALU.add, op1=ALU.max,
                                                         accum_out=mx[:, h, col:col + 1])
                else:
                    ins = nc.vector.reduce_max(mx[:, h, col:col + 1], ps, AX.X)
                inc(ins, maxes_used)
                if n % NMX == NMX - 1:
                    wait(dve, maxes_used, hp, u, n + 1)
                    inc(nc.vector.tensor_tensor(out=mx[:, h, 4:8], in0=mx[:, h, 4:8], in1=mx[:, h, 8:12], op=ALU.max),
                        mx_ready)

            def store_z(hp, u, h, half):
                ps = z_ps[half][:, 0:4 * (D + 1)].rearrange("p (t c) -> p t c", t=4)
                n = h * 2 + half + 1
                wait(dve, probs_used, hp, u, h * NPC + LAST_OF[half] + 1)
                inc(nc.vector.reciprocal(rden[:, half, :], ps[:, :, D]), rden_ready)
                if h == 0:
                    wait(dve, turn_ready["zT"], hp, u, half + 1 - 2)
                wait(dve, rden_ready, hp, u, n)
                ins = nc.vector.tensor_tensor(
                    out=z[:, h, 2 * half:2 * half + 2, :].rearrange("p t (c d) -> p (t c) d", c=2), in0=ps[:, :, 0:D],
                    in1=rden[:, half, :].unsqueeze(2).to_broadcast([P, 4, D]), op=ALU.mult)
                inc(ins, z_stored)

            def item(hp, kind, u, n):
                turn, par = (kind, u, n), u % 2
                if kind == "stats":
                    dve.wait_ge(s_x[n], 16)
                    for t in range(n * T, (n + 1) * T):
                        nc.vector.bn_stats(stats[:, t, :], x_sb[:, t, :]).then_inc(s["stats_done"], 1)
                    for t in range(n * T, (n + 1) * T):
                        dve.wait_ge(s["stats_done"], t + 1)
                        nc.vector.bn_aggr(mv[:, t, :], stats[:, t, :]).then_inc(s["mv_done"], 1)
                    dve.wait_ge(s["mv_done"], (n + 1) * T)
                    nc.vector.tensor_scalar(mv[:, n * T:(n + 1) * T, 1], mv[:, n * T:(n + 1) * T, 1], EPS, None,
                                            ALU.add).then_inc(s["var_eps_done"], 1)
                    if n == B - 1:
                        dve.wait_ge(s["gw_loaded"], 64)
                        nc.vector.tensor_reduce(kmax[:, 0:1], kw, AX.X, ALU.max, apply_absolute_value=True
                                                ).then_inc(s["kmax_ready"], 1)
                elif kind == "norm":
                    dve.wait_ge(s["rstd_done"], n + 1)
                    for t in range(n * T, (n + 1) * T):
                        nc.vector.tensor_scalar(xn[:, t, :], x_sb[:, t, :], mv[:, t, 0:1], mv[:, t, 1:2],
                                                ALU.subtract, ALU.mult).then_inc(s["xn_done"], 1)
                elif kind == "xT":
                    cols = slice(n * HALF, (n + 1) * HALF)
                    wait(dve, xT_hi_ready, hp, u, n + 1)
                    inc(nc.vector.tensor_tensor(out=xT_lo[:, cols], in0=turn_bank(turn)[:, :],
                                                in1=xT_hi[:, cols].bitcast(F32), op=ALU.subtract), xT_lo_ready)
                elif kind == "gk":
                    wait(dve, turn_ready[kind], hp, u, n + 1)
                    gk_part(n, turn_bank(turn))
                elif kind == "z":
                    store_z(hp, u, n // 2, n % 2)
                elif kind == "max":
                    row_max(hp, u, n)
                elif kind == "qk_lo":
                    which, half = n // 2, n % 2
                    cols = slice(half * HALF, (half + 1) * HALF)
                    wait(dve, hi_ready, hp, u, 2 * (n + 1))
                    if u % B == 0 and n == 0:
                        wait(dve, w_lo_ready, hp, u, 2)
                    for h in range(2):
                        hi = (QA, KA)[which][0:D, par, h, cols]
                        lo = (QB[0:D, par, h, cols], KA[D:P, par, h, cols])[which]
                        ins = nc.vector.scalar_tensor_tensor(out=lo, in0=turn_bank(("qk", u, n))[h * D:(h + 1) * D, :],
                                                             scalar=b_dve[:, which, h:h + 1], in1=hi.bitcast(F32),
                                                             op0=ALU.add, op1=ALU.subtract)
                    inc(ins, lo_ready)
                elif kind == "v_add":
                    wait(dve, turn_ready["v"], hp, u, n + 1)
                    wait(dve, v1_ready, hp, u, n + 1 - 2)
                    inc(nc.vector.scalar_tensor_tensor(
                        out=v_sb[:, n, :].rearrange("p (t c) -> p t c", t=4),
                        in0=turn_bank(("v", u, n))[:, :].rearrange("p (t c) -> p t c", t=4), scalar=v_scale[:, 0:1],
                        in1=bv_cur[:, :].unsqueeze(1).to_broadcast([P, 4, P]), op0=ALU.mult, op1=ALU.add), v_stored)
                elif kind == "v2":
                    wait(dve, v1_ready, hp, u, n + 1)
                    inc(nc.vector.tensor_tensor(out=V2[:, par, 4 * n:4 * n + 4, :, :], in0=by_head(v_sb[:, n, :]),
                                                in1=V1[:, par, 4 * n:4 * n + 4, :, 0:D], op=ALU.subtract), v2_ready)
                elif kind == "v_bound" and n == 0:
                    dve.wait_ge(s["wv_loaded"], 16)
                    then(nc.vector.tensor_reduce(v_max[:, 0:1], wv_all[:, :, :].rearrange("p c e -> p (c e)"), AX.X,
                                                 ALU.max, apply_absolute_value=True))
                    then(nc.vector.tensor_reduce(v_max[:, 1:2], bv_all[:, :], AX.X, ALU.max,
                                                 apply_absolute_value=True))
                    nc.vector.scalar_tensor_tensor(out=v_max[:, 2:3], in0=v_max[:, 0:1], scalar=float(E),
                                                   in1=v_max[:, 1:2], op0=ALU.mult, op1=ALU.add
                                                   ).then_inc(s["v_max_ready"], 1)
                    wait(dve, turn_ready[kind], hp, u, 1)
                    inc(nc.vector.reduce_max(v_max[0:1, 3:4], turn_bank(turn)[0:1, 0:P], AX.X), v_bound_used)
                elif kind == "v_bound":
                    wait(dve, turn_ready[kind], hp, u, 2)
                    inc(nc.vector.tensor_scalar(v_unscale[:, 0:1], turn_bank(turn)[:, 0:1], 1.0 / V_TOP, TINY,
                                                ALU.mult, ALU.max), v_bound_used)
                    wait(dve, v_bound_used, hp, u, 2)
                    then(nc.vector.reciprocal(v_scale[:, 0:1], v_unscale[:, 0:1]))
                    then(nc.vector.tensor_scalar(bv_all[:, :], bv_all[:, :], v_scale[:, 0:1], None, ALU.mult))
                    then(nc.vector.tensor_copy(bv_cur[:, :], bv_all[:, 0:P]))
                elif kind == "neg_max":
                    wait(dve, turn_ready["maxT"], hp, u, n + 1)
                    wait(dve, max_row[n], hp, u, 0)
                    inc(nc.vector.tensor_scalar(neg_max[:, n, :], turn_bank(("maxT", u, n))[0:T, 0:P], -1.0, SCALE * math.log(GAIN),
                                                ALU.mult, ALU.add), neg_max_ready)
                elif kind == "out":
                    wait(dve, turn_ready["proj"], hp, u, 1)
                    wait(dve, gate_stored, hp, u, 1)
                    wait(dve, out_written[par], hp, u, 0)
                    inc(nc.vector.tensor_tensor(out=out_sb[:, par, :], in0=turn_bank(("proj", u, 0))[:, 0:E],
                                                in1=gate_sb[:, :], op=ALU.mult), gated)
                    wait(dve, gated, hp, u, 1)
                    inc(nc.vector.tensor_tensor(out=out_sb[:, par, :], in0=out_sb[:, par, :],
                                                in1=x_sb[:, bass.ds(u % B * T + hp + u // B, 1), :], op=ALU.add),
                        out_ready)
                elif kind == "w":
                    cols = slice(0, 2 * P) if n == 0 else slice(2 * P, 3 * P)
                    pair = hp + u // B
                    if n == 0:
                        wait(dve, v_stored, hp, u - 1, 2)
                        nc.vector.tensor_copy(b_dve[:, :, :], b_all[:, :, bass.ds(pair * 2, 2)])
                        if u:
                            nc.vector.tensor_copy(bv_cur[:, :], bv_all[:, bass.ds(pair * P, P)])
                    wait(dve, w_hi_ready, hp, u, n + 1)
                    inc(nc.vector.tensor_tensor(out=wT_lo[:, cols], in0=turn_bank(turn)[:, 0:cols.stop - cols.start],
                                                in1=wT_hi[:, cols].bitcast(F32), op=ALU.subtract), w_lo_ready)
                elif kind == "g_y":
                    wait(dve, g_abs_ready, hp, u, 1)
                    wait(dve, turn_ready["gateT"], hp, u, 0)
                    inc(nc.vector.tensor_scalar(gT[:, :], turn_bank(("gate", u, 0))[:, 0:P], g_bias, None, ALU.add), g_steps)
                elif kind == "silu":
                    if n == 0:
                        wait(dve, g_exp_ready, hp, u, 1)
                        inc(nc.vector.tensor_scalar(g_den[:, :], g_exp[:, :], 1.0, None, ALU.add), g_steps)
                        wait(dve, g_steps, hp, u, 2)
                        inc(nc.vector.scalar_tensor_tensor(out=g_exp[:, :], in0=gT[:, :], scalar=0.0, in1=g_exp[:, :],
                                                           op0=ALU.is_ge, op1=ALU.max), g_steps)
                    elif n == 1:
                        inc(nc.vector.reciprocal(g_den[:, :], g_den[:, :]), g_steps)
                    else:
                        wait(dve, g_steps, hp, u, 4)
                        inc(nc.vector.tensor_tensor(out=gT[:, :], in0=gT[:, :], in1=g_exp[:, :], op=ALU.mult), g_steps)
                        wait(dve, g_steps, hp, u, 5)
                        inc(nc.vector.scalar_tensor_tensor(out=gT[:, :], in0=gT[:, :], scalar=v_unscale[:, 0:1],
                                                           in1=g_den[:, :], op0=ALU.mult, op1=ALU.mult), gT_ready)

            dve.wait_ge(s["consts_loaded"], 48)
            run(dve, item)

        @block.tensor
        def _(pe):
            mm = nc.tensor.matmul
            pe.wait_ge(s["ident_ready"], 1)
            def three(out, w_hi, w_lo, m_hi, m_lo, **kw):
                mm(out, w_hi, m_hi, start=True, stop=False, **kw)
                mm(out, w_hi, m_lo, start=False, stop=False, **kw)
                return mm(out, w_lo, m_hi, start=False, stop=True, **kw)

            def item(hp, kind, u, n):
                turn, b, par = (kind, u, n), u % B, u % 2
                if kind == "score":
                    h, k = n // NPC, n % NPC
                    ps = score_ps[n % 2]
                    if k == 0:
                        wait(pe, max_row[h], hp, u, 1)
                        if h == 0:
                            wait(pe, kB_filled, hp, u, 1)
                        if u == 0 and h == 0:
                            pe.wait_ge(s["fixed_ready"], 4)
                    wait(pe, probs_ready, hp, u, n + 1 - 2)
                    at = 0
                    for j, s0, w in PIECES[k]:
                        keys, queries = slice(j * P, (j + 1) * P), slice(s0 * P, (s0 + w) * P)
                        dst = ps[:, at:at + w * P]
                        mm(dst, KA[:, par, h, keys], QA[:, par, h, queries], start=True, stop=False)
                        last = mm(dst, KB[:, par, h, keys], QB[:, par, h, queries], start=False, stop=True)
                        at += w * P
                    inc(last, scores_ready)
                elif kind == "pv":
                    h, k = n // NPC, n % NPC
                    half = int(k >= FIRST_OF[1])
                    first = k == FIRST_OF[half]
                    if n == 0:
                        wait(pe, v2_ready, hp, u, 2)
                    if first:
                        wait(pe, z_stored, hp, u, h * 2 + half + 1 - 2)
                    wait(pe, p_lo_ready, hp, u, n + 1)
                    at = 0
                    for j, s0, w in PIECES[k]:
                        i = s0
                        while i < s0 + w:
                            alone = i % 2
                            width = (1 if alone else 2) * P
                            for odd in range(2):
                                c = (i // 2 % 2 * 2 + odd) * (D + 1)
                                dst = z_ps[half][D if alone else 0:P, c:c + D + 1]
                                cols = slice(at + odd, at + width, 2)
                                hi, lo = p_hi[:, n % PART_SLOTS, cols], p_lo[:, n % PART_SLOTS, cols]
                                v1, v2 = V1[:, par, j, h, :], V2[:, par, j, h, :]
                                products = [(hi, v1), (hi, v2), (lo, v1)]
                                for x, (p, v) in enumerate(products):
                                    last = mm(dst if v.shape[-1] == D + 1 else dst[:, 0:D], p, v, start=first,
                                              stop=x == len(products) - 1 and (j == i or j == i + 1),
                                              skip_group_check=True)
                                    first = False
                            at += width
                            i += 1 if alone else 2
                    inc(last, probs_used)
                elif kind in TURN_KINDS and kind != "spare":
                    if LAST_TURN[turn]:
                        name, before, at = freed(LAST_TURN[turn])
                        wait(pe, name, hp, before, at)
                    ps = turn_bank(turn)
                    if kind == "max":
                        h, (i, key0, keys, _) = n // NMX, MAXES[n % NMX]
                        if n in (0, 4):
                            wait(pe, lo_ready, hp, u, 4 if n else 3)
                        if n == 0:
                            wait(pe, qA_filled, hp, u, 1)
                        inc(mm(ps[:, 0:keys], QA[:, par, h, i * P:(i + 1) * P], KA[:, par, h, key0:key0 + keys],
                               start=True, stop=True), maxes_ready)
                        return
                    if kind == "qk":
                        which, half = n // 2, n % 2
                        if b == 0 and n == 0:
                            wait(pe, w_lo_ready, hp, u, 2)
                        if u == 0:
                            wait(pe, xT_lo_ready, 0, 0, n % 2 + 1)
                        if u == 1 and n == 0:
                            pe.wait_ge(count[xT_lo_ready][0], 2 * 2)
                        col0 = b * S + half * HALF
                        w = slice(which * P, (which + 1) * P)
                        last = three(ps[:, :], wT_hi[:, w], wT_lo[:, w], xT_hi[:, col0:col0 + HALF],
                                     xT_lo[:, col0:col0 + HALF])
                    elif kind == "v":
                        for i in range(4):
                            tok = b * S + (4 * n + i) * P
                            last = three(ps[:, i * P:(i + 1) * P], xT_hi[:, tok:tok + P], xT_lo[:, tok:tok + P],
                                         wT_hi[:, 2 * P:3 * P], wT_lo[:, 2 * P:3 * P])
                    elif kind == "maxT":
                        wait(pe, mx_ready, hp, u, n + 1)
                        last = nc.tensor.transpose(ps[0:T, 0:P], mx[:, n, 0:T], ident[:, :])
                    elif kind == "zT":
                        wait(pe, z_stored, hp, u, 2 + n + 1)
                        for tp in range(2):
                            for h in range(2):
                                c = (tp * 2 + h) * P
                                last = nc.tensor.transpose(ps[:, c:c + P], z[:, h, 2 * n + tp, :], ident[:, :])
                    elif kind == "proj":
                        wait(pe, zT_copied, hp, u, 2)
                        if u == 0:
                            pe.wait_ge(s["pj_loaded"], 16)
                        for c in range(8):
                            last = mm(ps[:, 0:E], zT[:, c, :, :].rearrange("p h a -> p (h a)"),
                                      pj[:, c * E:(c + 1) * E], start=c == 0, stop=c == 7)
                    elif kind == "w":
                        if n == 0:
                            wait(pe, w_loaded, hp, u, 3)
                        for i in (0, 1) if n == 0 else (2,):
                            c = (i % 2) * P
                            last = nc.tensor.transpose(ps[:, c:c + P], w_nat[:, i, :], ident[:, :])
                    elif kind == "gate":
                        if u == 0:
                            pe.wait_ge(s["gw_ready"], 1)
                        rows = bass.ds((hp + u // B) * P + b * S, P)
                        last = three(ps[:, 0:P], gw_hi[:, :], gw_lo[:, :], xT_hi[:, rows], xT_lo[:, rows])
                    elif kind == "gateT":
                        wait(pe, gT_ready, hp, u, 1)
                        last = nc.tensor.transpose(ps[:, 0:P], gT[:, :], ident[:, :])
                    elif kind == "xT":
                        pe.wait_ge(s["xn_done"], (n + 1) * 4)
                        for i in range(4):
                            last = nc.tensor.transpose(ps[:, i * P:(i + 1) * P], xn[:, n * 4 + i, :], ident[:, :])
                    elif kind == "v_bound":
                        if n == 0:
                            pe.wait_ge(s["v_max_ready"], 1)
                            last = nc.tensor.transpose(ps[0:1, 0:P], v_max[:, 2:3], ident[:, :])
                        else:
                            wait(pe, v_bound_used, 0, 0, 1)
                            pe.wait_ge(s["ones_ready"], 1)
                            last = mm(ps[:, 0:1], ones_row, v_max[0:1, 3:4], start=True, stop=True)
                    elif kind == "gk":
                        if n == 0:
                            pe.wait_ge(s["kmax_ready"], 1)
                            last = nc.tensor.transpose(ps[0:1, 0:P], kmax[:, 0:1], ident[:, :])
                        elif n == 1:
                            last = nc.tensor.transpose(ps[0:R, 0:P], la, ident[:, :])
                        elif n == 2:
                            wait(pe, gk_used, 0, 0, 1)
                            pe.wait_ge(s["ones_ready"], 1)
                            last = mm(ps[:, 0:1], ones_row, kmax_row[0:1, 0:1], start=True, stop=True)
                        else:
                            wait(pe, gk_used, 0, 0, 2)
                            last = mm(ps[:, 0:P], laT, lb, start=True, stop=True)
                    inc(last, turn_ready[kind])

            run(pe, item)


_INS = ["L0_attn_x", "L0_attn_Wq", "L0_attn_bq", "L0_attn_Wk", "L0_attn_bk", "L0_attn_Wv", "L0_attn_bv",
        "L0_attn_proj", "L0_ffn_kernel", "L0_ffn_bias", "L0_ffn_a", "L0_ffn_b"]


def kernel(**inputs):
    import numpy as _np
    import concourse.bacc as _bacc
    from concourse import mybir as _mybir
    from concourse.bass_utils import run_bass_kernel_spmd as _run

    nc = _bacc.Bacc("TRN2", target_bir_lowering=False, num_devices=1)
    arrays, args = {}, []
    for name in _INS:
        a = _np.ascontiguousarray(inputs[name])
        arrays[f"in_{name}_dram"] = a
        args.append(nc.dram_tensor(f"in_{name}_dram", a.shape, _mybir.dt.from_np(a.dtype), kind="ExternalInput").ap())
    args.append(nc.dram_tensor("out_dram", (B, S, E), _mybir.dt.float32, kind="ExternalOutput").ap())
    attention_kernel(nc, *args)
    r = _run(nc, [arrays], core_ids=[0])
    return r.results[0]["out_dram"]
```
